# Optimizing a Trainium2 kernel written in Bass

```python
import numpy as np
import jax
import jax.numpy as jnp

def _softmax(x, axis=-1):
    return jax.nn.softmax(x, axis=axis)

def _gelu(x):
    return jax.nn.gelu(x, approximate=True)

def _silu(x):
    return jax.nn.silu(x)

def _sigmoid(x):
    return jax.nn.sigmoid(x)

def _layernorm(x, axis=-1, eps=1e-05):
    m = jnp.mean(x, axis=axis, keepdims=True)
    v = jnp.var(x, axis=axis, keepdims=True)
    return (x - m) / jnp.sqrt(v + eps)

def _scatter_add(tgt, idx, src, axis=0):
    return tgt.at[idx].add(src)

def _segment_sum(src, seg, n):
    return jax.ops.segment_sum(src, seg, n)
kernel_name = 'mk_audio_tower_d2_tok_audfeat1024_r4_25f0c4'

def setup_inputs(seed: int=0):
    np.random.seed(seed)
    _w = jnp.asarray

    def _rec_inputs():
        import jax
        import jax.numpy as jnp
        _rk = jax.random.key(seed)
        x = -0.000125008 + 0.999885 * jax.random.normal(jax.random.fold_in(_rk, 1), (8, 128, 750), jnp.float32)
        return x
    x = _rec_inputs()

    def _L0_tok_setup():
        import jax, jax.numpy as jnp
        import numpy as np
        from jax import lax
        ALPHA = 0.1
        B, C_IN, T, D_MODEL = (32, 128, 512, 256)

        def _ewma_scan(xt):

            def step(carry, xi):
                carry = ALPHA * xi + (1.0 - ALPHA) * carry
                return (carry, carry)
            _, ys = lax.scan(step, xt[0], xt[1:])
            return jnp.concatenate([xt[:1], ys], axis=0)
        key = jax.random.key(seed)
        k_x, k_w, k_b = jax.random.split(key, 3)
        x = jax.random.normal(k_x, (B, C_IN, T), dtype=jnp.float32)
        bound = 1.0 / np.sqrt(C_IN)
        W = jax.random.uniform(k_w, (D_MODEL, C_IN), dtype=jnp.float32, minval=-bound, maxval=bound)
        b = jax.random.uniform(k_b, (D_MODEL,), dtype=jnp.float32, minval=-bound, maxval=bound)
        return {'x': x, 'W': W, 'b': b}
    _L0_tok_all = _L0_tok_setup()
    _L0_tok_in = {k: v for k, v in _L0_tok_all.items() if k in ('W', 'b')}
    del _L0_tok_all

    def _L0_attn_setup():
        import math
        import jax, jax.numpy as jnp
        import numpy as np
        B, S, D, H = (2, 512, 256, 16)
        HD = D // H
        key = jax.random.key(seed)
        k1, k2, k3 = jax.random.split(key, 3)
        h = jax.random.normal(k1, (B, S, D), dtype=jnp.float32)
        Wqvk = jax.random.normal(k2, (D, 3 * D), dtype=jnp.float32) * (1.0 / math.sqrt(D))
        Wo = jax.random.normal(k3, (D, D), dtype=jnp.float32) * (1.0 / math.sqrt(D))
        return {'h': h, 'Wqvk': Wqvk, 'Wo': Wo}
    _L0_attn_all = _L0_attn_setup()
    _L0_attn_in = {k: v for k, v in _L0_attn_all.items() if k in ('Wqvk', 'Wo')}
    del _L0_attn_all

    def _L0_ffn_setup():
        import jax, jax.numpy as jnp
        import numpy as np
        B, T, D, E, H = (8, 512, 256, 8, 64)
        LN_EPS = 1e-05
        key = jax.random.key(seed)
        ks = jax.random.split(key, 4)
        return {'x': jax.random.normal(ks[0], (B, T, D), dtype=jnp.float32), 'Wg': jax.random.normal(ks[1], (E, D), dtype=jnp.float32) * 0.02, 'ln_scale': jnp.ones((E, D), dtype=jnp.float32), 'ln_bias': jnp.zeros((E, D), dtype=jnp.float32), 'W1': jax.random.normal(ks[2], (E, D, H), dtype=jnp.float32) * 0.02, 'b1': jnp.zeros((E, H), dtype=jnp.float32), 'W2': jax.random.normal(ks[3], (E, H, D), dtype=jnp.float32) * 0.02, 'b2': jnp.zeros((E, D), dtype=jnp.float32)}
    _L0_ffn_all = _L0_ffn_setup()
    _L0_ffn_in = {k: v for k, v in _L0_ffn_all.items() if k in ('Wg', 'ln_scale', 'ln_bias', 'W1', 'b1', 'W2', 'b2')}
    del _L0_ffn_all

    def _L1_attn_setup():
        import jax, jax.numpy as jnp
        import numpy as np
        import math
        B, T, D, H = (2, 512, 256, 16)
        DH = D // H

        def rotate_half(x):
            x1 = x[..., ::2]
            x2 = x[..., 1::2]
            return jnp.stack((-x2, x1), axis=-1).reshape(x.shape)
        key = jax.random.key(seed)
        k1, k2, k3 = jax.random.split(key, 3)
        x = jax.random.normal(k1, (B, T, D), dtype=jnp.float32)
        Wqkv = jax.random.normal(k2, (3 * D, D), dtype=jnp.float32) * (1.0 / math.sqrt(D))
        Wo = jax.random.normal(k3, (D, D), dtype=jnp.float32) * (1.0 / math.sqrt(D))
        return {'x': x, 'Wqkv': Wqkv, 'Wo': Wo}
    _L1_attn_all = _L1_attn_setup()
    _L1_attn_in = {k: v for k, v in _L1_attn_all.items() if k in ('Wqkv', 'Wo')}
    del _L1_attn_all

    def _L1_ffn_setup():
        import jax, jax.numpy as jnp
        import numpy as np
        INT8_MAX = 127.0

        def _absmax_scale(x, axes):
            amax = jnp.max(jnp.abs(x), axis=axes, keepdims=True)
            return jnp.maximum(amax, 1e-12) / INT8_MAX
        key = jax.random.key(seed)
        k1, k2 = jax.random.split(key)
        lhs = jax.random.normal(k1, (4, 2048, 256), dtype=jnp.float32)
        rhs = jax.random.normal(k2, (256, 256), dtype=jnp.float32)
        return {'lhs': lhs, 'rhs': rhs}
    _L1_ffn_all = _L1_ffn_setup()
    _L1_ffn_in = {k: v for k, v in _L1_ffn_all.items() if k in ('rhs',)}
    del _L1_ffn_all
    return {'x': x, 'L0_tok_W': _L0_tok_in['W'], 'L0_tok_b': _L0_tok_in['b'], 'L0_attn_Wqvk': _L0_attn_in['Wqvk'], 'L0_attn_Wo': _L0_attn_in['Wo'], 'L0_ffn_Wg': _L0_ffn_in['Wg'], 'L0_ffn_ln_scale': _L0_ffn_in['ln_scale'], 'L0_ffn_ln_bias': _L0_ffn_in['ln_bias'], 'L0_ffn_W1': _L0_ffn_in['W1'], 'L0_ffn_b1': _L0_ffn_in['b1'], 'L0_ffn_W2': _L0_ffn_in['W2'], 'L0_ffn_b2': _L0_ffn_in['b2'], 'L1_attn_Wqkv': _L1_attn_in['Wqkv'], 'L1_attn_Wo': _L1_attn_in['Wo'], 'L1_ffn_rhs': _L1_ffn_in['rhs']}

def reference(x, L0_tok_W, L0_tok_b, L0_attn_Wqvk, L0_attn_Wo, L0_ffn_Wg, L0_ffn_ln_scale, L0_ffn_ln_bias, L0_ffn_W1, L0_ffn_b1, L0_ffn_W2, L0_ffn_b2, L1_attn_Wqkv, L1_attn_Wo, L1_ffn_rhs):
    import jax
    import jax.numpy as jnp

    def _L0_tok_ref(x, W, b):
        import jax, jax.numpy as jnp
        import numpy as np
        from jax import lax
        ALPHA = 0.1
        B, C_IN, T, D_MODEL = (32, 128, 512, 256)

        def _ewma_scan(xt):

            def step(carry, xi):
                carry = ALPHA * xi + (1.0 - ALPHA) * carry
                return (carry, carry)
            _, ys = lax.scan(step, xt[0], xt[1:])
            return jnp.concatenate([xt[:1], ys], axis=0)
        xp = jnp.transpose(x, (0, 2, 1))
        xt = jnp.moveaxis(xp, 1, 0)
        fwd = _ewma_scan(xt)
        bwd = _ewma_scan(xt[::-1])[::-1]
        ewma = jnp.moveaxis((fwd + bwd) * 0.5, 0, 1)
        return jnp.einsum('btc,dc->btd', ewma, W) + b

    def _L0_attn_ref(h, Wqvk, Wo):
        import math
        import jax, jax.numpy as jnp
        import numpy as np
        B, S, D, H = (2, 512, 256, 16)
        HD = D // H
        b, s, d = h.shape
        qvk = (h @ Wqvk).reshape(b, s, 3, H, HD)
        q, v, k = (qvk[:, :, 0], qvk[:, :, 1], qvk[:, :, 2])
        scores = jnp.einsum('bshi,bthi->bsth', q, k)
        mask = jnp.where(jnp.arange(s)[None, :] > jnp.arange(s)[:, None], jnp.float32(-jnp.inf), jnp.float32(0.0))
        scores = scores + mask[None, :, :, None]
        scores = scores / math.sqrt(d)
        weights = jax.nn.softmax(scores, axis=2)
        wv = jnp.einsum('bsth,bthi->bshi', weights, v).reshape(b, s, d)
        return wv @ Wo

    def _L0_ffn_ref(x, Wg, ln_scale, ln_bias, W1, b1, W2, b2):
        import jax, jax.numpy as jnp
        import numpy as np
        B, T, D, E, H = (8, 512, 256, 8, 64)
        LN_EPS = 1e-05
        Bs, Ts, Ds = x.shape
        xt = x.reshape(Bs * Ts, Ds)
        logits = xt @ Wg.T
        top1 = jnp.argmax(logits, axis=-1)
        mu = jnp.mean(xt, axis=-1, keepdims=True)
        var = jnp.mean(jnp.square(xt - mu), axis=-1, keepdims=True)
        xhat = (xt - mu) * jax.lax.rsqrt(var + LN_EPS)
        n_experts = Wg.shape[0]

        def body(y, p):
            s_e, b_e, w1, bb1, w2, bb2, eid = p
            h = jax.nn.gelu((xhat * s_e + b_e) @ w1 + bb1, approximate=False)
            out = h @ w2 + bb2
            mask = (top1 == eid)[:, None].astype(out.dtype)
            return (y + mask * out, None)
        y0 = jnp.zeros_like(xt)
        y, _ = jax.lax.scan(body, y0, (ln_scale, ln_bias, W1, b1, W2, b2, jnp.arange(n_experts)))
        return y.reshape(Bs, Ts, Ds)

    def _L1_attn_ref(x, Wqkv, Wo):
        import jax, jax.numpy as jnp
        import numpy as np
        import math
        B, T, D, H = (2, 512, 256, 16)
        DH = D // H

        def rotate_half(x):
            x1 = x[..., ::2]
            x2 = x[..., 1::2]
            return jnp.stack((-x2, x1), axis=-1).reshape(x.shape)
        b, t, d = x.shape
        pos = jnp.arange(t, dtype=jnp.float32)
        freqs = jnp.exp(-math.log(10000.0) * jnp.arange(0, DH, 2, dtype=jnp.float32) / DH)
        angles = pos[:, None] * freqs[None, :]
        angles = jnp.repeat(angles, 2, axis=-1)
        sin = jnp.sin(angles)[None, None, :, :]
        cos = jnp.cos(angles)[None, None, :, :]
        qkv = x @ Wqkv.T
        q, k, v = jnp.split(qkv, 3, axis=-1)
        q = q.reshape(b, t, H, DH).transpose(0, 2, 1, 3)
        k = k.reshape(b, t, H, DH).transpose(0, 2, 1, 3)
        v = v.reshape(b, t, H, DH).transpose(0, 2, 1, 3)
        q = cos * q + rotate_half(q) * sin
        k = cos * k + rotate_half(k) * sin
        scores = jnp.einsum('bhqd,bhkd->bhqk', q, k) / math.sqrt(DH)
        causal = jnp.tril(jnp.ones((t, t), dtype=bool))
        scores = jnp.where(causal, scores, -jnp.inf)
        attn = jax.nn.softmax(scores, axis=-1)
        out = jnp.einsum('bhqk,bhkd->bhqd', attn, v)
        out = out.transpose(0, 2, 1, 3).reshape(b, t, d)
        return out @ Wo.T

    def _L1_ffn_ref(lhs, rhs):
        import jax, jax.numpy as jnp
        import numpy as np
        INT8_MAX = 127.0

        def _absmax_scale(x, axes):
            amax = jnp.max(jnp.abs(x), axis=axes, keepdims=True)
            return jnp.maximum(amax, 1e-12) / INT8_MAX
        lhs_scale = _absmax_scale(lhs, (2,))
        rhs_scale = _absmax_scale(rhs, (0,))
        q_lhs = jnp.clip(jnp.round(lhs / lhs_scale), -INT8_MAX, INT8_MAX).astype(jnp.int8)
        q_rhs = jnp.clip(jnp.round(rhs / rhs_scale), -INT8_MAX, INT8_MAX).astype(jnp.int8)
        acc = jax.lax.dot_general(q_lhs, q_rhs, (((2,), (0,)), ((), ())), preferred_element_type=jnp.int32)
        return acc.astype(jnp.float32) * lhs_scale * rhs_scale
    h = _L0_tok_ref(x, L0_tok_W, L0_tok_b)
    h = h + _L0_attn_ref(_layernorm(h, axis=-1), L0_attn_Wqvk, L0_attn_Wo)
    h = h + _L0_ffn_ref(_layernorm(h, axis=-1), L0_ffn_Wg, L0_ffn_ln_scale, L0_ffn_ln_bias, L0_ffn_W1, L0_ffn_b1, L0_ffn_W2, L0_ffn_b2)
    h = h + _L1_attn_ref(_layernorm(h, axis=-1), L1_attn_Wqkv, L1_attn_Wo)
    h = h + _L1_ffn_ref(_layernorm(h, axis=-1), L1_ffn_rhs)
    return h

_drawn_inputs = setup_inputs


def setup_inputs(seed=0):
    import zlib

    import numpy as np

    out = dict(_drawn_inputs(seed))
    spreads = {'L0_ffn_ln_scale': (1.0, 0.6),
     'L0_ffn_ln_bias': (0.0, 0.8),
     'L0_ffn_b1': (0.0, 0.489),
     'L0_ffn_b2': (0.0, 0.1)}
    factors = {}
    for name, (base, spread) in spreads.items():
        noise = np.random.default_rng([zlib.crc32(name.encode()), seed]).standard_normal(out[name].shape)
        drawn = base * np.exp(spread * noise) if base else spread * noise
        out[name] = jnp.asarray(drawn.astype(out[name].dtype))
    for name, factor in factors.items():
        out[name] = (out[name] * factor).astype(out[name].dtype)
    return out
```

```python
from contextlib import ExitStack

import numpy as np

import concourse.bass as bass
from concourse import mybir

F32 = mybir.dt.float32
BF16 = mybir.dt.bfloat16
ALU = mybir.AluOpType
ACT = mybir.ActivationFunctionType
AX = mybir.AxisListType

B, C_IN, T = 8, 128, 750
D, H, DH = 256, 16, 16
E, HID = 8, 64
TB = 125
NT = T // TB
HALF = T // 2
KC = D // 128
GH = 4
NG = H // GH
HPC = 128 // DH
ALPHA = 0.1
EPS = 1e-5
MAGIC = 1.5 * 2.0 ** 23
INT8_MAX = 127.0
NEG = -1e30
Q_PARTS = (0, 0, 1, 1, 0, 2)
K_PARTS = (0, 1, 0, 1, 2, 0)
NSTRIP = len(Q_PARTS)
KROWS = NSTRIP * DH
SROWS = KROWS + 3

MAX_UNITS = ([(0, 0, 4), (1, 0, 4)] + [(i, j, 2) for i in (2, 3) for j in (0, 2)]
             + [(i, j, 1) for i in (4, 5) for j in range(4)])
CHUNKS = [
    [(0, 0, 500, 0)],
    [(0, 500, 750, 0), (1, 500, 750, 250)],
    [(1, 125, 500, 0), (5, 625, 750, 375)],
    [(2, 250, 750, 0)],
    [(3, 375, 750, 0)],
    [(4, 500, 750, 0)],
]
NCH = len(CHUNKS)
WIDTH = [sum(q1 - q0 for _, q0, q1, _ in ch) for ch in CHUNKS]
DIAGONAL = [0, None, (0, 375), 0, 0, 0]
NMASKED = sum(d is not None for d in DIAGONAL) * GH
CUT = 500
RING = 3
LEAD = 7
LAYERS = 2
NORMS = 5


def attention_order():
    ahead = []
    for g in range(NG):
        ahead += [("max", g, u) for u in range(len(MAX_UNITS))]
    for g in range(NG):
        at = min((g + 1) * len(MAX_UNITS) + 2, NG * len(MAX_UNITS)) + g
        ahead.insert(at, ("shift", g))
    order, at = [], len(MAX_UNITS) + 1 + LEAD
    order += ahead[:at]
    per = -(-(len(ahead) - at) // ((NG - 1) * NCH))
    for g in range(NG):
        for c in range(NCH):
            order.append(("chunk", g, c))
            order += ahead[at:at + per]
            at += per
            if c == 2 and g > 0:
                order.append(("turn", g - 1))
    order.append(("turn", NG - 1))
    return order


ORDER = attention_order()


def slot_uses():
    uses = [("tok", n) for n in range(3)]

    def turned(what):
        return [(what, c) for c in range(KC)]

    for layer in range(LAYERS):
        uses += turned(("xt", 1 if layer == 0 else 4))
        if layer == 0:
            uses += [("qk", layer, w, c) for w in range(2) for c in range(KC)]
        else:
            uses += [("qktok", n) for n in range(3)]
        uses += [("v", layer, n) for n in range(2)]
        if layer == 1:
            uses += [("qk", layer, w, c) for w in range(2) for c in range(KC)]
        uses += [("att", layer) + o for o in ORDER if o[0] != "chunk"]
        uses += turned(("ao", layer))
        uses += [("wo", layer, n) for n in range(2)]
        if layer == 0:
            uses += turned(("xt", 2))
            uses += [("logit",)]
            uses += turned(("xt", 3))
            uses += [("mask",)]
            uses += [("w1", m) for m in range(4)]
            uses += [("w2", n) for n in range(2)]
    uses += [("xt", 5, "q"), ("ffn", 0), ("ffn", 1)]
    return uses


USES = {key: k for k, key in enumerate(slot_uses())}
PER_SLOT = ((len(USES) + 1) // 2, len(USES) // 2)


def tower(nc, x, W, b, Wqvk, Wo0, Wg, ln_scale, ln_bias, W1, b1, W2, b2, Wqkv, Wo1, rhs,
          ident, causal, cosines, sines, pick, out):
    ctx = ExitStack()
    with ctx:
        def sb(name, shape, dt=F32):
            return ctx.enter_context(nc.sbuf_tensor(name, shape, dt))

        def sem(name):
            return ctx.enter_context(nc.semaphore(name))

        probs_raw = sb("probs", [128, RING * GH * CUT])
        probs = probs_raw[0:TB, :].rearrange("p (r n) -> p r n", n=CUT)
        early = [0]

        def early_weight(rows, *dims):
            n = int(np.prod(dims))
            v = probs_raw[0:rows, early[0]:early[0] + n]
            early[0] += n
            letters = "abcd"[:len(dims)]
            names = {c: d for c, d in zip(letters, dims)}
            return v.rearrange(f"p ({' '.join(letters)}) -> p {' '.join(letters)}", **names) if len(dims) > 1 else v

        pickf = early_weight(32, 4, 128)
        w_tok = early_weight(128, KC, 128)
        w_g = early_weight(E, D)
        lns = early_weight(E, 2, D)
        w_1 = early_weight(128, KC, E, HID)
        b_2r = early_weight(E, D)
        w_raw = early_weight(128, 6, D)
        w_o1 = early_weight(128, KC, D)
        rhs_t = early_weight(128, KC, D)
        r_diag = early_weight(128, KC, 128)
        assert early[0] <= RING * GH * CUT

        identf = sb("identf", [128, 128])
        identb = sb("identb", [128, 128], BF16)
        maskf = sb("maskf", [TB, TB])
        maskb = sb("maskb", [TB, TB], BF16)
        cos_sb = sb("cos_sb", [TB, NT, DH])
        sin_sb = sb("sin_sb", [TB, NT, DH])
        pickb = sb("pickb", [32, 4, 128], BF16)
        decay = sb("decay", [128, T])
        ones = sb("ones", [128, TB])
        neghalf = sb("neghalf", [TB, NT])
        rank = sb("rank", [TB, E])
        wt_tok = sb("wt_tok", [128, D])
        b_tok = sb("b_tok", [TB, D])
        w_qvk = sb("w_qvk", [128, KC, 3 * D])
        w_o0 = sb("w_o0", [128, KC, D])
        wt_g = sb("wt_g", [128, KC, E])
        lnt = sb("lnt", [128, 2, KC, E])
        w_1s = sb("w_1s", [128, KC, E * HID])
        b_1 = sb("b_1", [128, 4])
        b_1e = sb("b_1e", [128, 4])
        w_2 = sb("w_2", [128, 4, D])
        b_2 = sb("b_2", [E, D])
        b_2p = sb("b_2p", [E, 3, D], BF16)
        b_2s = sb("b_2s", [32, D], BF16)
        w_qkv = sb("w_qkv", [128, KC, 3 * D])
        w_o1t = sb("w_o1t", [128, KC, D])
        r_abs = sb("r_abs", [128, 3, KC])
        rq_t = sb("rq_t", [128, KC, D], BF16)
        rq = sb("rq", [128, KC, D], BF16)
        r_scale = sb("r_scale", [TB, D])

        xin = sb("xin", [128, T])
        fwd = sb("fwd", [128, T])
        res = sb("res", [TB, NT, D])
        stats = sb("stats", [TB, NT, 6])
        mv = sb("mv", [TB, NT, 2])
        veps = sb("veps", [TB, NT])
        rstd = sb("rstd", [TB, NT])
        xn = sb("xn", [TB, NT, D])
        xh = sb("xh", [TB, NT, D])
        xt = sb("xt", [128, KC, T])
        rest = sb("rest", [128, 2, T])
        xs, bwd = rest[:, 0, :], rest[:, 1, :]
        parts = sb("parts", [128, 2, 3, KC, T], BF16)
        qp = sb("qp", [SROWS, H, T], BF16)
        kp = sb("kp", [SROWS, H, T], BF16)
        va = sb("va", [TB, NT, H, 32])
        mx = sb("mx", [TB, 2, GH, NT])
        ms = sb("ms", [TB, 2, 3, GH * NT], BF16)
        mr = sb("mr", [TB, GH * NT])
        mt = sb("mt", [3 * GH * NT, 2, TB], BF16)
        os_ = sb("os", [128, T])
        rden = sb("rden", [TB, NT, GH])
        rot = sb("rot", [TB, 2, 2 * D])
        hidden = sb("hidden", [128, NT * 2 * D])
        ghid = hidden[:, 0:4 * T].rearrange("p (m t) -> p m t", m=4)
        qr = hidden[0:TB, :].rearrange("p (t n) -> p t n", t=NT)
        lg = sb("lg", [TB, NT, E])
        lgm = sb("lgm", [TB, 2, NT])
        sel = sb("sel", [TB, NT, E])
        mk = sb("mk", [TB, NT, 32], BF16)
        mkt = sb("mkt", [32, NT, TB], BF16)
        am = sb("am", [TB, 3, NT])
        qb = sb("qb", [TB, NT, D], BF16)
        qbt = sb("qbt", [128, KC, T], BF16)

        slot = [ctx.enter_context(nc.psum_tensor(f"slot{i}", [128, 2, 512], F32)) for i in range(2)]
        st = [ctx.enter_context(nc.psum_tensor(f"st{i}", [128, 512], F32)) for i in range(2)]
        acc = ctx.enter_context(nc.psum_tensor("acc", [128, 2, 512], F32))
        slotb = [s[:].bitcast(BF16) for s in slot]
        stb = [s[:].bitcast(BF16) for s in st]

        signals = []

        class Signal:

            def __init__(self, name, per):
                self.sem, self.per = sem(name), per
                signals.append(self)

        turn = {}

        def need(eng, signal, n):
            eng.wait_ge(signal.sem, turn[eng] * signal.per + (n + 1))
            if eng in stands_apart:
                stand_apart(eng)

        stands_apart = []

        def stand_apart(eng):
            eng.sem_inc(s_waited, 1)

        full = [Signal(f"slot{i}_full", PER_SLOT[i]) for i in range(2)]
        done = [Signal(f"slot{i}_done", PER_SLOT[i]) for i in range(2)]
        s_weights = sem("weights_loaded")
        s_setup = {n: sem(f"setup_{n}") for n in ("pool", "act", "dve", "pe", "b2", "side")}
        s_x = Signal("x_loaded", 16)
        s_xs = Signal("x_scaled", 1)
        s_scan = Signal("scanned", 2)
        s_ends = Signal("scan_ends", 2)
        s_ewma = Signal("ewma_ready", 1)
        s_stats = Signal("norm_stats", NORMS)
        s_mv = Signal("norm_moments", NORMS)
        s_veps = Signal("norm_veps", NORMS)
        s_rstd = Signal("norm_rstd", NORMS)
        s_norm = Signal("normalised", NORMS * NT)
        s_high = Signal("part_high", LAYERS * 2 * KC)
        s_rest = Signal("part_rest", LAYERS * 2 * KC)
        s_mid = Signal("part_mid", LAYERS * 2 * KC)
        s_lowq = Signal("part_low", LAYERS * 2 * KC)
        s_packed = Signal("packed", LAYERS * 2 * NSTRIP * HPC * 16)
        s_ms = Signal("shift_parts", LAYERS * NG * 4)
        s_mrow = [Signal(f"shift_row{i}", LAYERS * (NG // 2) * 3 * 16) for i in range(2)]
        s_scores = Signal("scores_ready", LAYERS * NG * NCH * GH)
        s_exp = Signal("exp_done", LAYERS * NG * NCH * GH)
        s_masked = Signal("masked", LAYERS * NG * NMASKED)
        s_pv = Signal("values_summed", LAYERS * NG * NCH)
        s_osb = Signal("sums_copied", LAYERS * NG)
        s_rden = Signal("denominators", LAYERS * NG)
        s_qr = Signal("rotary_done", NT)
        s_gate = Signal("gate_steps", 5)
        s_mk = Signal("gate_masks", 2)
        s_amax = Signal("quant_scale", 3)
        s_quant = Signal("quant_steps", NT + 2)
        s_out = Signal("result_ready", 1)
        s_stored = Signal("stored", 16)

        def await_done(eng, *keys, free=None):
            at = {}
            for k in [USES[key] for key in keys] + ([] if free is None else [USES[free] - 2]):
                at[k % 2] = max(at.get(k % 2, 0), k // 2 + 1)
            for i, n in at.items():
                need(eng, done[i], n)

        def take(eng, key, *results):
            await_done(eng, *results, free=key)
            return slot[USES[key] % 2]

        def filled(ins, key):
            ins.then_inc(full[USES[key] % 2].sem, 1)

        def await_full(eng, key):
            k = USES[key]
            need(eng, full[k % 2], k // 2 + 1)
            return slot[k % 2]

        def consumed(ins, key):
            ins.then_inc(done[USES[key] % 2].sem, 1)

        weights = [
            (identf[:], ident), (maskf[:], causal),
            (cos_sb[:], cosines.rearrange("(t p) d -> p t d", p=TB)),
            (sin_sb[:], sines.rearrange("(t p) d -> p t d", p=TB)),
            (pickf[:], pick),
            (w_tok[:], W.rearrange("(c p) i -> p c i", p=128)),
            (b_tok[:], b.partition_broadcast(TB)),
            (w_qvk[:], Wqvk.rearrange("(c p) n -> p c n", p=128)),
            (w_o0[:], Wo0.rearrange("(c p) n -> p c n", p=128)),
            (w_g[:], Wg), (lns[:, 0, :], ln_scale), (lns[:, 1, :], ln_bias),
            (b_2[:], b2),
            (w_2[:], W2.rearrange("(c e) h n -> (e h) c n", e=2)),
            (w_raw[:], Wqkv.rearrange("(c p) n -> p c n", p=128)),
            (w_o1[:], Wo1.rearrange("(c p) n -> p c n", p=128)),
            (rhs_t[:], rhs.rearrange("(c p) n -> p c n", p=128)),
        ]
        for c in range(KC):
            weights.append((w_1[:, c], W1.rearrange("e (c p) h -> c p e h", p=128)[c]))
        for c in range(4):
            weights.append((b_1[:, c:c + 1], b1.rearrange("(c e) h -> c (e h)", e=2)[c].rearrange("(p a) -> p a", a=1)))
        n_weights = 16 * len(weights)
        s_waited = sem("waited")

        block = ctx.enter_context(nc.Block())

        @block.sync
        def _(sp):
            for dst, src in weights:
                sp.dma_start(dst, src).then_inc(s_weights, 16)
            for signal in signals:
                sp.sem_inc(signal.sem, 1)
            sp.wait_ge(s_setup["dve"], 11)
            sp.wait_ge(s_setup["pool"], 5)
            for p in range(3):
                sp.dma_start(b_2s[p * E:(p + 1) * E, :], b_2p[:, p, :]).then_inc(s_setup["b2"], 16)
            xv = x
            ov = out.rearrange("b (t p) d -> b p t d", p=TB)
            stands_apart.append(sp)
            with sp.Fori(0, B) as i:
                turn[sp] = i
                need(sp, s_ends, 0)
                need(sp, s_scan, 0)
                sp.dma_start(xin[:], xv[bass.ds(i, 1)].rearrange("a c t -> (a c) t")).then_inc(s_x.sem, 16)

                for layer in range(LAYERS):
                    for w in range(2):
                        dst = (qp, kp)[w]
                        if layer:
                            need(sp, s_pv, NG * NCH)
                        else:
                            need(sp, s_pv, 0)
                        need(sp, s_lowq, (layer * 2 + w + 1) * KC)
                        for strip, part in enumerate((Q_PARTS, K_PARTS)[w]):
                            for h in range(HPC):
                                sp.dma_start(
                                    dst[strip * DH:(strip + 1) * DH, h::HPC, :],
                                    parts[h * DH:(h + 1) * DH, w, part, :, :],
                                ).then_inc(s_packed.sem, 16)
                    for g in range(NG):
                        await_done(sp, ("att", layer, "shift", g))
                        for p in range(3):
                            n = GH * NT
                            sp.dma_start(
                                qp[KROWS + p:KROWS + p + 1, g * GH:(g + 1) * GH, :],
                                mt[p * n:(p + 1) * n, g % 2, :],
                            ).then_inc(s_mrow[g % 2].sem, 16)
                need(sp, s_out, 1)
                sp.dma_start(ov[bass.ds(i, 1)].rearrange("a p t d -> p (a t) d"), res[:]).then_inc(s_stored.sem, 16)
            sp.wait_ge(s_stored.sem, B * 16 + 1)

        @block.tensor
        def _(pe):
            mm = nc.tensor.matmul

            def setup():
                pe.wait_ge(s_weights, n_weights)
                pe.wait_ge(s_setup["pool"], 7)
                a = slot[0]
                for c in range(KC):
                    last = nc.tensor.transpose(a[:, 0, c * 128:(c + 1) * 128], w_tok[:, c, :], identf[:])
                last.then_inc(s_setup["pe"], 1)
                for c in range(KC):
                    cols = slice(c * 128, (c + 1) * 128)
                    nc.tensor.transpose(a[:, 1, c * 8:c * 8 + 8], w_g[:, cols], identf[0:E, 0:E])
                    for v in range(2):
                        o = 16 + v * 16 + c * 8
                        last = nc.tensor.transpose(a[:, 1, o:o + 8], lns[:, v, cols], identf[0:E, 0:E])
                last.then_inc(s_setup["pe"], 1)
                for c in range(KC):
                    s = slot[1]
                    if c:
                        pe.wait_ge(s_setup["act"], 3)
                    for r in range(6):
                        last = nc.tensor.transpose(s[:, r // 3, r % 3 * 128:r % 3 * 128 + 128],
                                                   w_raw[:, r, c * 128:(c + 1) * 128], identf[:])
                    last.then_inc(s_setup["pe"], 1)
                for c in range(KC):
                    for r in range(KC):
                        last = nc.tensor.transpose(st[0][:, (c * KC + r) * 128:(c * KC + r + 1) * 128],
                                                   w_o1[:, r, c * 128:(c + 1) * 128], identf[:])
                last.then_inc(s_setup["pe"], 1)
                for c in range(KC):
                    for r in range(KC):
                        last = nc.tensor.transpose(st[1][:, (c * KC + r) * 128:(c * KC + r + 1) * 128],
                                                   rhs_t[:, r, c * 128:(c + 1) * 128], identf[:])
                last.then_inc(s_setup["pe"], 1)
                pe.wait_ge(s_setup["act"], 2)
                for e in range(E):
                    for c in range(KC):
                        last = mm(acc[64 * (e % 2):64 * (e % 2) + 64, 0, e // 2:e // 2 + 1],
                                  w_1[:, c, e, :], lnt[:, 1, c, e:e + 1], start=(c == 0), stop=(c == KC - 1))
                last.then_inc(s_setup["pe"], 1)
                pe.wait_ge(s_setup["dve"], 8)
                pe.wait_ge(s_setup["act"], 5)
                for c in range(KC):
                    for r in range(KC):
                        last = nc.tensor.transpose(stb[0][:, (c * KC + r) * 128:(c * KC + r + 1) * 128],
                                                   rq_t[:, r, c * 128:(c + 1) * 128], identb[:])
                last.then_inc(s_setup["pe"], 1)
                for c in range(KC):
                    last = mm(acc[0:TB, 1, c * 128:(c + 1) * 128], ones[:], r_diag[:, c, :], start=True, stop=True)
                last.then_inc(s_setup["pe"], 1)
                pe.wait_ge(s_setup["dve"], 12)
                pe.wait_ge(s_setup["act"], 8)
                pe.wait_ge(s_setup["b2"], 48)

            def turned(key, src, norm):
                for c in range(KC):
                    s = take(pe, (key, c))
                    for t in range(NT):
                        if c == 0:
                            need(pe, s_norm, norm * NT + t + 1)
                        last = nc.tensor.transpose(s[:, t // 3, t % 3 * TB:t % 3 * TB + TB],
                                                   src[:, t, c * 128:(c + 1) * 128], identf[0:TB, 0:TB])
                    filled(last, (key, c))

            def attention(layer):
                heads = layer * NG * NCH * GH
                sent = [0, 0]

                def max_unit(g, u):
                    i, h0, nh = MAX_UNITS[u]
                    key = ("att", layer, "max", g, u)
                    s = take(pe, key)
                    n = (i + 1) * TB
                    for j in range(nh):
                        h = g * GH + h0 + j
                        q = qp[0:KROWS, h, i * TB:(i + 1) * TB]
                        if nh == 4:
                            per = 4 if i == 0 else 2
                            pieces = [(j // per, j % per * n, 0, n)]
                        elif nh == 2:
                            pieces = [(j, 0, 0, n)]
                        else:
                            w = -(-n // 2)
                            pieces = [(0, 0, 0, w), (1, 0, n - w, n)]
                        for bank, col, k0, k1 in pieces:
                            diag = k1 == n
                            last = mm(s[0:TB, bank, col:col + k1 - k0], q, kp[0:KROWS, h, k0:k1],
                                      start=True, stop=not diag, skip_group_check=True)
                            if diag:
                                at = col + n - TB - k0
                                last = mm(s[0:TB, bank, at:at + TB], identb[0:TB, 0:TB], maskb[:],
                                          start=False, stop=True, skip_group_check=True)
                    filled(last, key)

                def shift(g):
                    key = ("att", layer, "shift", g)
                    s = take(pe, key)
                    need(pe, s_ms, (layer * NG + g + 1) * 4)
                    n = 3 * GH * NT
                    filled(nc.tensor.transpose(slotb[USES[key] % 2][0:n, 0, 0:TB],
                                               ms[:, g % 2, :, :].rearrange("p a b -> p (a b)"),
                                               identb[0:TB, 0:TB]), key)

                def scores(g, c):
                    for j in range(GH):
                        n = heads + (g * NCH + c) * GH + j
                        h = g * GH + j
                        if n >= 2:
                            need(pe, s_exp, n - 1)
                        else:
                            need(pe, s_exp, 0)
                        for kb, q0, q1, col in CHUNKS[c]:
                            last = mm(st[n % 2][0:TB, col:col + q1 - q0], kp[:, h, kb * TB:(kb + 1) * TB],
                                      qp[:, h, q0:q1], start=True, stop=True, skip_group_check=True)
                        last.then_inc(s_scores.sem, 1)

                def values(g, c):
                    chunk = (layer * NG + g) * NCH + c
                    if DIAGONAL[c] is None:
                        need(pe, s_exp, (chunk + 1) * GH)
                    else:
                        before = sum(d is not None for d in DIAGONAL[:c + 1]) * GH
                        need(pe, s_masked, (layer * NG + g) * NMASKED + before)
                    if g == 0 and c == 0:
                        await_done(pe, ("v", layer, 0), ("v", layer, 1))
                    if c == 0:
                        need(pe, s_osb, layer * NG + g)
                    for kb, q0, q1, col in CHUNKS[c]:
                        for a, z in ((q0, min(q1, CUT)), (max(q0, CUT), q1)):
                            if a >= z:
                                continue
                            bank = a >= CUT
                            for j in range(GH):
                                ring = chunk % RING * GH + j
                                last = mm(acc[32 * j:32 * j + 32, int(bank), a - CUT * bank:z - CUT * bank],
                                          va[:, kb, g * GH + j, :],
                                          probs[:, ring, col + a - q0:col + z - q0],
                                          start=(kb == 0), stop=False, skip_group_check=True)
                    last.then_inc(s_pv.sem, 1)

                def turn_sums(g):
                    key = ("att", layer, "turn", g)
                    s = take(pe, key)
                    need(pe, s_osb, layer * NG + g + 1)
                    for t in range(NT):
                        last = nc.tensor.transpose(s[0:TB, t // 3, t % 3 * 128:t % 3 * 128 + 128],
                                                   os_[:, t * TB:(t + 1) * TB], identf[:])
                    filled(last, key)

                need(pe, s_packed, (layer + 1) * 2 * NSTRIP * HPC * 16)
                late = None
                for o in ORDER:
                    if o[0] == "max":
                        max_unit(o[1], o[2])
                    elif o[0] == "shift":
                        shift(o[1])
                    elif o[0] == "turn":
                        if o[1] == NG - 1:
                            values(*late)
                            late = None
                        turn_sums(o[1])
                    else:
                        g, c = o[1], o[2]
                        if c == 0:
                            need(pe, s_mrow[g % 2], (layer * (NG // 2) + g // 2 + 1) * 48)
                        scores(g, c)
                        if late is not None:
                            values(*late)
                        late = (g, c)

            def project(layer, w_o):
                for c in range(KC):
                    key = (("ao", layer), c)
                    s = take(pe, key, ("att", layer, "turn", NG - 1))
                    for t in range(NT):
                        last = nc.tensor.transpose(s[:, t // 3, t % 3 * TB:t % 3 * TB + TB],
                                                   xn[:, t, c * 128:(c + 1) * 128], identf[0:TB, 0:TB])
                    filled(last, key)
                by_blocks([("wo", layer, n) for n in range(2)], both(("ao", layer)), xt, lambda c: w_o[:, c, :], KC)

            def both(key):
                return [(key, c) for c in range(KC)]

            def by_blocks(keys, after, lhs, rhs_of, nk, more=None):
                for n, key in enumerate(keys):
                    s = take(pe, key, *after)
                    for j in range(3):
                        t = n * 3 + j
                        o = s[0:TB, j // 2, j % 2 * D:j % 2 * D + D]
                        for c in range(nk):
                            last = mm(o, lhs[:, c, t * TB:(t + 1) * TB], rhs_of(c), start=(c == 0),
                                      stop=(c == nk - 1 and more is None))
                        if more is not None:
                            last = mm(o, more[0][:, t, :], more[1], start=False, stop=True)
                    filled(last, key)

            def features_by(key, after, weight, extra=None):
                s = take(pe, key, *after)
                for half in range(2):
                    for c in range(KC):
                        last = mm(s[:, half, 0:HALF], weight(c), xt[:, c, half * HALF:(half + 1) * HALF],
                                  start=(c == 0), stop=(c == KC - 1 and extra is None))
                    if extra is not None:
                        last = mm(s[:, half, 0:HALF], extra,
                                  mkt[:, half * 3:half * 3 + 3, :].rearrange("p a b -> p (a b)"), start=False, stop=True)
                filled(last, key)

            setup()
            with pe.Fori(0, B) as i:
                turn[pe] = i
                need(pe, s_ewma, 1)
                for n in range(3):
                    s = take(pe, ("tok", n))
                    for j in range(2):
                        t = n * 2 + j
                        last = mm(s[0:TB, j, 0:D], fwd[:, t * TB:(t + 1) * TB], wt_tok[:], start=True, stop=True)
                    filled(last, ("tok", n))
                turned(("xt", 1), xn, 0)
                for w in range(2):
                    for c in range(KC):
                        col = w * 2 * D + c * 128
                        features_by(("qk", 0, w, c), both(("xt", 1)), lambda k, col=col: w_qvk[:, k, col:col + 128])
                by_blocks([("v", 0, n) for n in range(2)], [], xt, lambda c: w_qvk[:, c, D:2 * D], KC)
                attention(0)
                project(0, w_o0)
                turned(("xt", 2), xn, 1)
                s = take(pe, ("logit",), *both(("xt", 2)))
                for t in range(NT):
                    for c in range(KC):
                        last = mm(s[0:TB, 0, t * E:(t + 1) * E], xt[:, c, t * TB:(t + 1) * TB], wt_g[:, c, :],
                                  start=(c == 0), stop=(c == KC - 1))
                filled(last, ("logit",))
                turned(("xt", 3), xh, 2)
                s = take(pe, ("mask",))
                need(pe, s_mk, 2)
                for t in range(NT):
                    last = nc.tensor.transpose(slotb[USES[("mask",)] % 2][0:32, 0, t * 128:t * 128 + TB],
                                               mk[:, t, :], identb[0:TB, 0:TB])
                filled(last, ("mask",))
                for m in range(4):
                    features_by(("w1", m), [("mask",), *both(("xt", 3))], lambda k, m=m: w_1s[:, k, m * 128:(m + 1) * 128], pickb[:, m, :])
                by_blocks([("w2", n) for n in range(2)], [("w1", m) for m in range(4)], ghid, lambda c: w_2[:, c, :], 4, (mkt, b_2s[:]))
                turned(("xt", 4), xn, 3)
                for n in range(3):
                    s = take(pe, ("qktok", n), *both(("xt", 4)))
                    for j in range(2):
                        t = n * 2 + j
                        for c in range(KC):
                            last = mm(s[0:TB, j, :], xt[:, c, t * TB:(t + 1) * TB], w_qkv[:, c, 0:2 * D],
                                      start=(c == 0), stop=(c == KC - 1))
                    filled(last, ("qktok", n))
                by_blocks([("v", 1, n) for n in range(2)], [], xt, lambda c: w_qkv[:, c, 2 * D:3 * D], KC)
                for w in range(2):
                    for c in range(KC):
                        s = take(pe, ("qk", 1, w, c))
                        for t in range(NT):
                            need(pe, s_qr, t + 1)
                            col = w * D + c * 128
                            last = nc.tensor.transpose(s[:, t // 3, t % 3 * TB:t % 3 * TB + TB],
                                                       qr[:, t, col:col + 128], identf[0:TB, 0:TB])
                        filled(last, ("qk", 1, w, c))
                attention(1)
                project(1, w_o1t)
                key = ("xt", 5, "q")
                s = take(pe, key)
                need(pe, s_quant, NT + 2)
                for c in range(KC):
                    for t in range(NT):
                        last = nc.tensor.transpose(slotb[USES[key] % 2][:, c, t * 128:t * 128 + TB],
                                                   qb[:, t, c * 128:(c + 1) * 128], identb[0:TB, 0:TB])
                filled(last, key)
                by_blocks([("ffn", n) for n in range(2)], [key], qbt, lambda c: rq[:, c, :], KC)

        @block.scalar
        def _(act):
            def copy(o, i):
                return nc.scalar.activation(o, i, ACT.Copy)

            def setup():
                act.wait_ge(s_setup["pe"], 1)
                nc.scalar.mul(wt_tok[:], slot[0][:, 0, 0:D], 0.5).then_inc(s_setup["act"], 1)
                act.wait_ge(s_setup["pe"], 2)
                copy(wt_g[:].rearrange("p c e -> p (c e)"), slot[0][:, 1, 0:16])
                copy(lnt[:].rearrange("p a c e -> p (a c e)"), slot[0][:, 1, 16:48]).then_inc(s_setup["act"], 1)
                for c in range(KC):
                    act.wait_ge(s_setup["pe"], 3 + c)
                    copy(w_qkv[:, c, :].rearrange("p (a n) -> p a n", a=2), slot[1][:, :, 0:384])\
                        .then_inc(s_setup["act"], 1)
                act.wait_ge(s_setup["pe"], 5)
                copy(w_o1t[:].rearrange("p c n -> p (c n)"), st[0][:]).then_inc(s_setup["act"], 1)
                act.wait_ge(s_setup["pe"], 7)
                nc.scalar.activation(b_1e[:], acc[:, 0, 0:4], ACT.Copy).then_inc(s_setup["act"], 1)
                act.wait_ge(s_setup["pe"], 8)
                copy(rq[:].rearrange("p c n -> p (c n)"), stb[0][:, 0:2 * D]).then_inc(s_setup["act"], 1)
                act.wait_ge(s_setup["pe"], 9)
                copy(r_scale[:], acc[0:TB, 1, 0:D]).then_inc(s_setup["act"], 1)

            def copy_turned(key):
                for c in range(KC):
                    s = await_full(act, (key, c))
                    consumed(copy(xt[:, c, :].rearrange("p (a n) -> p a n", a=2), s[:, :, 0:HALF]), (key, c))

            def copy_v(layer):
                for n in range(2):
                    s = await_full(act, ("v", layer, n))
                    copy(va[:, n * 3:n * 3 + 2, :, 0:DH],
                         s[0:TB, 0, :].rearrange("p (t h d) -> p t h d", t=2, h=H))
                    consumed(copy(va[:, n * 3 + 2, :, 0:DH],
                                  s[0:TB, 1, 0:D].rearrange("p (h d) -> p h d", h=H)), ("v", layer, n))

            def high_parts(layer):
                for w in range(2):
                    for c in range(KC):
                        s = await_full(act, ("qk", layer, w, c))
                        need(act, s_packed, layer * 2 * NSTRIP * HPC * 16)
                        copy(parts[:, w, 0, c, :].rearrange("p (a n) -> p a n", a=2), s[:, :, 0:HALF])\
                            .then_inc(s_high.sem, 1)

            def attention(layer):
                scale = 1.0 / 16.0 if layer == 0 else 0.25
                for o in ORDER:
                    if o[0] == "shift":
                        key = ("att", layer) + o
                        g = o[1]
                        await_full(act, key)
                        need(act, s_mrow[g % 2], (layer * (NG // 2) + g // 2) * 48)
                        consumed(copy(mt[:, g % 2, :], slotb[USES[key] % 2][0:3 * GH * NT, 0, 0:TB]), key)
                    elif o[0] == "chunk":
                        g, c = o[1], o[2]
                        chunk = (layer * NG + g) * NCH + c
                        for j in range(GH):
                            n = chunk * GH + j
                            need(act, s_scores, n + 1)
                            need(act, s_pv, max(chunk - RING + 1, 0))
                            nc.scalar.activation(probs[:, chunk % RING * GH + j, 0:WIDTH[c]],
                                                 st[n % 2][0:TB, 0:WIDTH[c]], ACT.Exp, scale=scale)\
                                .then_inc(s_exp.sem, 1)
                        if c == 0 and g > 0:
                            copy_sums(layer, g - 1)
                copy_sums(layer, NG - 1)

            def copy_sums(layer, g):
                need(act, s_pv, (layer * NG + g + 1) * NCH)
                if g > 0:
                    await_full(act, ("att", layer, "turn", g - 1))
                copy(os_[:, 0:CUT], acc[:, 0, 0:CUT])
                copy(os_[:, CUT:T], acc[:, 1, 0:T - CUT]).then_inc(s_osb.sem, 1)

            setup()
            with act.Fori(0, B) as i:
                turn[act] = i
                need(act, s_x, 16)
                need(act, s_scan, 2)
                copy(fwd[:, 0:1], xin[:, 0:1]).then_inc(s_ends.sem, 1)
                copy(bwd[:, T - 1:T], xin[:, T - 1:T]).then_inc(s_ends.sem, 1)
                copy_turned(("xt", 1))
                high_parts(0)
                copy_v(0)
                attention(0)
                copy_turned(("ao", 0))
                copy_turned(("xt", 2))
                copy_turned(("xt", 3))
                s = await_full(act, ("mask",))
                k = USES[("mask",)]
                consumed(copy(mkt[:], slotb[k % 2][0:32, 0, 0:NT * 128].rearrange("p (t n) -> p t n", t=NT)[:, :, 0:TB]),
                         ("mask",))
                for m in range(4):
                    s = await_full(act, ("w1", m))
                    consumed(nc.scalar.activation(ghid[:, m, :].rearrange("p (a n) -> p a n", a=2), s[:, :, 0:HALF],
                                                  ACT.Gelu, bias=b_1[:, m:m + 1]), ("w1", m))
                copy_turned(("xt", 4))
                copy_v(1)
                high_parts(1)
                attention(1)
                copy_turned(("ao", 1))
                key = ("xt", 5, "q")
                await_full(act, key)
                consumed(copy(qbt[:].rearrange("p c (t n) -> p c t n", t=NT),
                              slotb[USES[key] % 2][:, :, 0:NT * 128].rearrange("p c (t n) -> p c t n", t=NT)[:, :, :, 0:TB]),
                         key)

        @block.gpsimd
        def _(pool):
            def setup():
                g = nc.gpsimd
                g.memset(decay[:], 1.0 - ALPHA).then_inc(s_setup["pool"], 1)
                g.memset(ones[:], 1.0).then_inc(s_setup["pool"], 1)
                g.memset(neghalf[:], -0.5).then_inc(s_setup["pool"], 1)
                g.memset(va[:], 0.0).then_inc(s_setup["pool"], 1)
                g.memset(b_2s[:], 0.0).then_inc(s_setup["pool"], 1)
                pool.wait_ge(s_setup["pool"], 5)
                g.memset(va[:, :, :, DH:DH + 1], 1.0).then_inc(s_setup["pool"], 1)
                for e in range(E):
                    last = g.memset(rank[:, e:e + 1], float(E - e))
                last.then_inc(s_setup["pool"], 1)

            def norm(n):
                need(pool, s_mv, n + 1)
                nc.gpsimd.tensor_scalar(veps[:], mv[:, :, 1], EPS, None, ALU.add).then_inc(s_veps.sem, 1)
                need(pool, s_veps, n + 1)
                nc.gpsimd.tensor_tensor(rstd[:], veps[:], neghalf[:], ALU.pow).then_inc(s_rstd.sem, 1)

            def low_parts(layer):
                for w in range(2):
                    for c in range(KC):
                        n = (layer * 2 + w) * KC + c
                        need(pool, s_mid, n + 1)
                        need(pool, s_packed, layer * 2 * NSTRIP * HPC * 16)
                        nc.gpsimd.tensor_tensor(parts[:, w, 2, c, :], rest[:, n % 2, :], parts[:, w, 1, c, :],
                                                ALU.subtract).then_inc(s_lowq.sem, 1)

            def attention(layer):
                for g in range(NG):
                    for c in range(NCH):
                        if DIAGONAL[c] is None:
                            continue
                        chunk = (layer * NG + g) * NCH + c
                        for j in range(GH):
                            need(pool, s_exp, chunk * GH + j + 1)
                            p = probs[:, chunk % RING * GH + j, :]
                            if c == 2:
                                v, pattern = p[:, 0:500].rearrange("p (a n) -> p a n", a=4)[:, 0::3, :], [[0, 2], [1, TB]]
                            else:
                                v, pattern = p[:, 0:TB], [[1, TB]]
                            nc.gpsimd.affine_select(out=v, in_=v, compare_op=ALU.is_ge, fill=0.0, base=0,
                                                    pattern=pattern, channel_multiplier=-1).then_inc(s_masked.sem, 1)

            setup()
            stands_apart.append(pool)
            with pool.Fori(0, B) as i:
                turn[pool] = i
                norm(0)
                low_parts(0)
                attention(0)
                norm(1)
                norm(2)
                norm(3)
                for t in range(NT):
                    if t % 2 == 0:
                        await_done(pool, ("qktok", t // 2))
                    nc.gpsimd.tensor_tensor(qr[:, t, :], qr[:, t, :], rot[:, t % 2, :], ALU.add).then_inc(s_qr.sem, 1)
                low_parts(1)
                attention(1)
                norm(4)

        @block.vector
        def _(dve):
            v = nc.vector

            def setup():
                n = s_setup["dve"]
                s_b2c = s_setup["side"]
                dve.wait_ge(s_weights, n_weights)
                v.tensor_copy(identb[:], identf[:]).then_inc(n, 1)
                v.tensor_copy(maskb[:], maskf[:]).then_inc(n, 1)
                v.memset(kp[KROWS:SROWS, :, :], 1.0)
                v.tensor_copy(pickb[:], pickf[:]).then_inc(n, 1)
                dve.wait_ge(s_setup["pe"], 6)
                src = st[1][:].rearrange("p (c n) -> p c n", c=KC)
                v.tensor_reduce(r_abs[:, 0, :], src, AX.X, ALU.max, apply_absolute_value=True).then_inc(n, 1)
                dve.wait_ge(n, 4)
                v.tensor_scalar(r_abs[:, 1, :], r_abs[:, 0, :], 1e-12, 1.0 / INT8_MAX, ALU.max, ALU.mult).then_inc(n, 1)
                dve.wait_ge(n, 5)
                v.reciprocal(r_abs[:, 2, :], r_abs[:, 1, :]).then_inc(n, 1)
                dve.wait_ge(n, 6)
                for c in range(KC):
                    v.tensor_scalar(rhs_t[:, c, :], src[:, c, :], r_abs[:, 2, c:c + 1], INT8_MAX, ALU.mult, ALU.min)
                    last = v.tensor_scalar(r_diag[:, c, :], identf[:], r_abs[:, 1, c:c + 1], None, ALU.mult)
                last.then_inc(n, 1)
                dve.wait_ge(n, 7)
                v.tensor_scalar(rhs_t[:], rhs_t[:], -INT8_MAX, MAGIC, ALU.max, ALU.add).then_inc(s_b2c, 1)
                dve.wait_ge(s_b2c, 1)
                v.tensor_scalar(rq_t[:], rhs_t[:], MAGIC, None, ALU.subtract).then_inc(n, 1)
                v.tensor_copy(b_2p[:, 0, :], b_2[:]).then_inc(s_b2c, 1)
                dve.wait_ge(s_b2c, 2)
                v.tensor_tensor(b_2r[:], b_2[:], b_2p[:, 0, :], ALU.subtract).then_inc(n, 1)
                dve.wait_ge(n, 9)
                v.tensor_copy(b_2p[:, 1, :], b_2r[:]).then_inc(n, 1)
                dve.wait_ge(n, 10)
                v.tensor_tensor(b_2p[:, 2, :], b_2r[:], b_2p[:, 1, :], ALU.subtract).then_inc(n, 1)
                dve.wait_ge(s_setup["act"], 6)
                for c in range(KC):
                    for e in range(E):
                        v.tensor_scalar(w_1s[:, c, e * HID:(e + 1) * HID], w_1[:, c, e, :],
                                        lnt[:, 0, c, e:e + 1], None, ALU.mult)
                v.tensor_tensor(b_1[:], b_1[:], b_1e[:], ALU.add).then_inc(n, 1)
                dve.wait_ge(s_setup["act"], 8)
                dve.wait_ge(s_setup["pool"], 7)

            def norm(n, src, dst, ready=None):
                for t in range(NT):
                    if ready is not None:
                        ready(t)
                    last = v.bn_stats(stats[:, t, :], src[:, t, :])
                last.then_inc(s_stats.sem, 1)
                need(dve, s_stats, n + 1)
                stand_apart(dve)
                for t in range(NT):
                    last = v.bn_aggr(mv[:, t, :], stats[:, t, :])
                last.then_inc(s_mv.sem, 1)
                need(dve, s_rstd, n + 1)
                for t in range(NT):
                    v.tensor_scalar(dst[:, t, :], src[:, t, :], mv[:, t, 0:1], rstd[:, t:t + 1],
                                    ALU.subtract, ALU.mult).then_inc(s_norm.sem, 1)

            def add_slots(keys, extra=None):
                for n, key in enumerate(keys):
                    s = await_full(dve, key)
                    a, z = res[:, n * 3:n * 3 + 2, :], res[:, n * 3 + 2, :]
                    v.tensor_tensor(a, s[0:TB, 0, :].rearrange("p (t d) -> p t d", t=2), a, ALU.add)
                    consumed(v.tensor_tensor(z, s[0:TB, 1, 0:D], z, ALU.add), key)

            def lower_parts(layer):
                for w in range(2):
                    for c in range(KC):
                        n = (layer * 2 + w) * KC + c
                        key = ("qk", layer, w, c)
                        s = await_full(dve, key)
                        need(dve, s_high, n + 1)
                        if n >= 2:
                            need(dve, s_lowq, n - 1)
                        else:
                            need(dve, s_lowq, 0)
                        two = "p (a n) -> p a n"
                        consumed(v.tensor_tensor(rest[:, n % 2, :].rearrange(two, a=2), s[:, :, 0:HALF],
                                                 parts[:, w, 0, c, :].rearrange(two, a=2), ALU.subtract), key)
                        await_done(dve, key)
                        v.tensor_copy(parts[:, w, 1, c, :], rest[:, n % 2, :]).then_inc(s_mid.sem, 1)

            def attention(layer):
                for o in ORDER:
                    key = ("att", layer) + o
                    if o[0] == "max":
                        g, u = o[1], o[2]
                        i, h0, nh = MAX_UNITS[u]
                        s = await_full(dve, key)
                        n = (i + 1) * TB
                        if i == 0:
                            src = s[0:TB, 0, 0:4 * n].rearrange("p (h t) -> p h t", h=4)
                        elif i == 1:
                            src = s[0:TB, :, 0:2 * n].rearrange("p b (h t) -> p b h t", h=2)
                        else:
                            src = s[0:TB, :, 0:(n if nh == 2 else -(-n // 2))]
                        consumed(v.tensor_reduce(mx[:, g % 2, h0:h0 + nh, i], src,
                                                 AX.XY if nh == 1 else AX.X, ALU.max), key)
                        if u == len(MAX_UNITS) - 1:
                            split_maxima(layer, g)
                    elif o[0] == "turn":
                        g = o[1]
                        n = layer * NG + g
                        s = await_full(dve, key)
                        if g > 0:
                            await_done(dve, ("att", layer, "turn", g - 1))
                        sv = s[0:TB, :, 0:384].rearrange("p b (t h f) -> p b t h f", t=3, h=GH)
                        for bk in range(2):
                            last = v.reciprocal(rden[:, 3 * bk:3 * bk + 3, :], sv[:, bk, :, :, DH])
                        last.then_inc(s_rden.sem, 1)
                        need(dve, s_rden, n + 1)
                        for bk in range(2):
                            last = v.tensor_tensor(
                                xn[:, 3 * bk:3 * bk + 3, g * 64:(g + 1) * 64].rearrange("p t (h d) -> p t h d", h=GH),
                                sv[:, bk, :, :, 0:DH],
                                rden[:, 3 * bk:3 * bk + 3, :].unsqueeze(3).broadcast_to([TB, 3, GH, DH]), ALU.mult)
                        consumed(last, key)

            def split_maxima(layer, g):
                base = (layer * NG + g) * 4
                await_done(dve, ("att", layer, "max", g, len(MAX_UNITS) - 1))
                m = mx[:, g % 2].rearrange("p h i -> p (h i)")
                v.tensor_scalar(ms[:, g % 2, 0, :], m, -1.0, None, ALU.mult).then_inc(s_ms.sem, 1)
                need(dve, s_ms, base + 1)
                v.scalar_tensor_tensor(out=mr[:], in0=m, scalar=-1.0, in1=ms[:, g % 2, 0, :],
                                       op0=ALU.mult, op1=ALU.subtract).then_inc(s_ms.sem, 1)
                need(dve, s_ms, base + 2)
                v.tensor_copy(ms[:, g % 2, 1, :], mr[:]).then_inc(s_ms.sem, 1)
                need(dve, s_ms, base + 3)
                v.tensor_tensor(ms[:, g % 2, 2, :], mr[:], ms[:, g % 2, 1, :], ALU.subtract).then_inc(s_ms.sem, 1)

            setup()
            with dve.Fori(0, B) as i:
                turn[dve] = i
                need(dve, s_x, 16)
                v.tensor_scalar(xs[:], xin[:], ALPHA, None, ALU.mult).then_inc(s_xs.sem, 1)
                need(dve, s_xs, 1)
                v.tensor_tensor_scan(fwd[:, 1:T], decay[:, 1:T], xs[:, 1:T], xin[:, 0:1],
                                     ALU.mult, ALU.add).then_inc(s_scan.sem, 1)
                v.tensor_tensor_scan(bwd[:, 0:T - 1][:, ::-1], decay[:, 1:T], xs[:, 0:T - 1][:, ::-1],
                                     xin[:, T - 1:T], ALU.mult, ALU.add).then_inc(s_scan.sem, 1)
                need(dve, s_scan, 2)
                need(dve, s_ends, 2)
                v.tensor_tensor(fwd[:], fwd[:], bwd[:], ALU.add).then_inc(s_ewma.sem, 1)
                need(dve, s_stored, 0)
                for n in range(3):
                    s = await_full(dve, ("tok", n))
                    consumed(v.tensor_tensor(res[:, 2 * n:2 * n + 2, :], s[0:TB, :, 0:D],
                                             b_tok[:].unsqueeze(1).broadcast_to([TB, 2, D]), ALU.add), ("tok", n))
                await_done(dve, ("tok", 2))
                norm(0, res, xn)
                lower_parts(0)
                attention(0)
                add_slots([("wo", 0, n) for n in range(2)])
                await_done(dve, ("wo", 0, 1))
                norm(1, res, xn)
                norm(2, xn, xh, lambda t: need(dve, s_norm, NT + t + 1))
                s = await_full(dve, ("logit",))
                consumed(v.tensor_copy(lg[:], s[0:TB, 0, 0:NT * E].rearrange("p (t e) -> p t e", t=NT)), ("logit",))
                await_done(dve, ("logit",))
                v.tensor_reduce(lgm[:, 0, :], lg[:], AX.X, ALU.max).then_inc(s_gate.sem, 1)
                need(dve, s_gate, 1)
                v.tensor_tensor(sel[:], lg[:], lgm[:, 0, :].unsqueeze(2).broadcast_to([TB, NT, E]), ALU.is_equal)\
                    .then_inc(s_gate.sem, 1)
                need(dve, s_gate, 2)
                v.tensor_tensor(sel[:], sel[:], rank[:].unsqueeze(1).broadcast_to([TB, NT, E]), ALU.mult).then_inc(s_gate.sem, 1)
                need(dve, s_gate, 3)
                v.tensor_reduce(lgm[:, 1, :], sel[:], AX.X, ALU.max).then_inc(s_gate.sem, 1)
                need(dve, s_gate, 4)
                v.tensor_tensor(sel[:], sel[:], lgm[:, 1, :].unsqueeze(2).broadcast_to([TB, NT, E]), ALU.is_equal)\
                    .then_inc(s_gate.sem, 1)
                need(dve, s_gate, 5)
                for r in range(3):
                    last = v.tensor_copy(mk[:, :, r * E:(r + 1) * E], sel[:])
                last.then_inc(s_mk.sem, 1)
                v.tensor_scalar(mk[:, :, 3 * E:4 * E], sel[:], -NEG, NEG, ALU.mult, ALU.add).then_inc(s_mk.sem, 1)
                add_slots([("w2", n) for n in range(2)])
                await_done(dve, ("w2", 1))
                norm(3, res, xn)
                for n in range(3):
                    key = ("qktok", n)
                    s = await_full(dve, key)
                    need(dve, s_qr, 2 * n)
                    for j in range(2):
                        t = 2 * n + j
                        v.tensor_tensor(qr[:, t, :].rearrange("p (h d) -> p h d", d=DH),
                                        s[0:TB, j, :].rearrange("p (h d) -> p h d", d=DH),
                                        cos_sb[:, t, :].unsqueeze(1).broadcast_to([TB, 2 * H, DH]), ALU.mult)
                        pairs = "p (h f two) -> p h f two"
                        last = v.tensor_tensor(
                            rot[:, j, :].rearrange(pairs, f=DH // 2, two=2),
                            s[0:TB, j, :].rearrange(pairs, f=DH // 2, two=2)[:, :, :, ::-1],
                            sin_sb[:, t, :].rearrange("p (f two) -> p f two", two=2).unsqueeze(1)
                            .broadcast_to([TB, 2 * H, DH // 2, 2]), ALU.mult)
                    consumed(last, key)
                lower_parts(1)
                attention(1)
                add_slots([("wo", 1, n) for n in range(2)])
                await_done(dve, ("wo", 1, 1))
                norm(4, res, xn)
                need(dve, s_norm, NORMS * NT)
                v.tensor_reduce(am[:, 0, :], xn[:], AX.X, ALU.max, apply_absolute_value=True).then_inc(s_amax.sem, 1)
                need(dve, s_amax, 1)
                v.tensor_scalar(am[:, 1, :], am[:, 0, :], 1e-12, 1.0 / INT8_MAX, ALU.max, ALU.mult).then_inc(s_amax.sem, 1)
                need(dve, s_amax, 2)
                v.reciprocal(am[:, 2, :], am[:, 1, :]).then_inc(s_amax.sem, 1)
                need(dve, s_amax, 3)
                for t in range(NT):
                    v.tensor_scalar(xh[:, t, :], xn[:, t, :], am[:, 2, t:t + 1], INT8_MAX, ALU.mult, ALU.min)\
                        .then_inc(s_quant.sem, 1)
                need(dve, s_quant, NT)
                v.tensor_scalar(xh[:], xh[:], -INT8_MAX, MAGIC, ALU.max, ALU.add).then_inc(s_quant.sem, 1)
                need(dve, s_quant, NT + 1)
                v.tensor_scalar(qb[:], xh[:], MAGIC, None, ALU.subtract).then_inc(s_quant.sem, 1)
                for n in range(2):
                    key = ("ffn", n)
                    s = await_full(dve, key)
                    for j in range(3):
                        t = n * 3 + j
                        last = v.scalar_tensor_tensor(out=xh[:, t, :], in0=s[0:TB, j // 2, j % 2 * D:j % 2 * D + D],
                                                      scalar=am[:, 1, t:t + 1], in1=r_scale[:],
                                                      op0=ALU.mult, op1=ALU.mult)
                    consumed(last, key)
                await_done(dve, ("ffn", 1))
                v.tensor_tensor(res[:], res[:], xh[:], ALU.add).then_inc(s_out.sem, 1)


_IN = ['x', 'L0_tok_W', 'L0_tok_b', 'L0_attn_Wqvk', 'L0_attn_Wo', 'L0_ffn_Wg', 'L0_ffn_ln_scale', 'L0_ffn_ln_bias',
       'L0_ffn_W1', 'L0_ffn_b1', 'L0_ffn_W2', 'L0_ffn_b2', 'L1_attn_Wqkv', 'L1_attn_Wo', 'L1_ffn_rhs']


def _tables():
    pos = np.arange(T, dtype=np.float32)
    freqs = np.exp(np.float32(-np.log(10000.0)) * np.arange(0, DH, 2, dtype=np.float32) / np.float32(DH))
    angles = np.repeat(pos[:, None] * freqs.astype(np.float32)[None, :], 2, axis=-1)
    sign = np.tile(np.array([-1.0, 1.0], np.float32), DH // 2)
    causal = np.where(np.arange(TB)[None, :] > np.arange(TB)[:, None], np.float32(NEG), np.float32(0.0))
    pick = np.zeros((32, 4, 128), np.float32)
    for e in range(E):
        pick[3 * E + e, e // 2, e % 2 * HID:(e % 2 + 1) * HID] = 1.0
    return {
        "ident": np.eye(128, dtype=np.float32), "causal": causal.astype(np.float32),
        "cosines": np.cos(angles).astype(np.float32), "sines": (np.sin(angles) * sign).astype(np.float32),
        "pick": pick,
    }


def kernel(**inputs):
    import concourse.bacc as _bacc
    from concourse.bass_utils import run_bass_kernel_spmd as _run

    nc = _bacc.Bacc("TRN2", target_bir_lowering=False, num_devices=1)
    arrays = {f"in_{n}": np.ascontiguousarray(inputs[n]) for n in _IN}
    arrays |= {f"table_{n}": a for n, a in _tables().items()}
    args = [nc.dram_tensor(n, a.shape, mybir.dt.from_np(a.dtype), kind="ExternalInput").ap() for n, a in arrays.items()]
    out = nc.dram_tensor("out", (B, T, D), F32, kind="ExternalOutput").ap()
    tower(nc, *args, out)
    r = _run(nc, [arrays], core_ids=[0])
    return r.results[0]["out"]
```

```python
from contextlib import ExitStack

import numpy as np

import concourse.bass as bass
from concourse import mybir

F32 = mybir.dt.float32
BF16 = mybir.dt.bfloat16
ALU = mybir.AluOpType
ACT = mybir.ActivationFunctionType
AX = mybir.AxisListType

B, C_IN, T = 8, 128, 750
D, H, DH = 256, 16, 16
E, HID = 8, 64
TB = 125
NT = T // TB
HALF = T // 2
KC = D // 128
GH = 4
NG = H // GH
HPC = 128 // DH
ALPHA = 0.1
EPS = 1e-5
MAGIC = 1.5 * 2.0 ** 23
INT8_MAX = 127.0
NEG = -1e30
Q_PARTS = (0, 0, 1, 1, 0, 2)
K_PARTS = (0, 1, 0, 1, 2, 0)
NSTRIP = len(Q_PARTS)
KROWS = NSTRIP * DH
SROWS = KROWS + 3

MAX_UNITS = ([(0, 0, 4), (1, 0, 4)] + [(i, j, 2) for i in (2, 3) for j in (0, 2)]
             + [(i, j, 1) for i in (4, 5) for j in range(4)])
CHUNKS = [
    [(0, 0, 500, 0)],
    [(0, 500, 750, 0), (1, 500, 750, 250)],
    [(1, 125, 500, 0), (5, 625, 750, 375)],
    [(2, 250, 750, 0)],
    [(3, 375, 750, 0)],
    [(4, 500, 750, 0)],
]
NCH = len(CHUNKS)
WIDTH = [sum(q1 - q0 for _, q0, q1, _ in ch) for ch in CHUNKS]
DIAGONAL = [0, None, (0, 375), 0, 0, 0]
NMASKED = sum(d is not None for d in DIAGONAL) * GH
CUT = 500
RING = 3
LEAD = 7
FILL = 0.8


def attention_order():
    ahead = []
    for g in range(NG):
        ahead += [("max", g, u) for u in range(len(MAX_UNITS))]
    for g in range(NG):
        at = min((g + 1) * len(MAX_UNITS) + 2, NG * len(MAX_UNITS)) + g
        ahead.insert(at, ("shift", g))
    order, at = [], len(MAX_UNITS) + 1 + LEAD
    order += ahead[:at]
    per = -(-(len(ahead) - at) // ((NG - 1) * NCH))
    for g in range(NG):
        for c in range(NCH):
            order.append(("chunk", g, c))
            order += ahead[at:at + per]
            at += per
            if c == 2 and g > 0:
                order.append(("turn", g - 1))
    order += [("last", NG - 1), ("turn", NG - 1)]
    return order


SLOTTED = ("max", "shift", "turn", "tok", "xt", "qk", "v", "ao", "wo", "logit", "mask", "w1", "w2", "qktok", "qt", "ffn")


class Affine:

    def __init__(self, k, c):
        self.k, self.c = k, c

    def __add__(self, n):
        return Affine(self.k, self.c + n)

    def times(self, n):
        return Affine(self.k * n, self.c * n)


class Step:
    def __init__(self, kind, layer, sample, *at):
        self.kind, self.layer, self.sample, self.at = kind, layer, sample, at
        self.key = (kind, layer) + at


def pre(b):
    return ([Step("scan", 0, b)] + [Step("tok", 0, b, n) for n in range(3)] + [Step("stash", 0, b)]
            + to_qkv(0, b))


def norm(layer, b, n):
    return [Step("stats", layer, b, n), Step("apply", layer, b, n)]


def to_qkv(layer, b):
    n = 3 * layer
    steps = norm(layer, b, n) + [Step("xt", layer, b, n, c) for c in range(KC)]
    if layer == 0:
        steps += [Step("qk", 0, b, w, c) for w in range(2) for c in range(KC)]
    else:
        steps += [Step("qktok", 1, b, n) for n in range(3)]
    steps += [Step("v", layer, b, n) for n in range(2)]
    if layer == 1:
        steps += [Step("qk", 1, b, w, c) for w in range(2) for c in range(KC)]
    return steps


def project(layer, b):
    return ([Step("fetch", layer, b)] + [Step("ao", layer, b, c) for c in range(KC)]
            + [Step("wo", layer, b, n) for n in range(2)])


def mid(b):
    return (project(0, b) + norm(0, b, 1) + [Step("xt", 0, b, 1, c) for c in range(KC)] + norm(0, b, 2)
            + [Step("logit", 0, b), Step("gate", 0, b)] + [Step("xt", 0, b, 2, c) for c in range(KC)]
            + [Step("mask", 0, b), Step("experts", 0, b)] + [Step("w2", 0, b, n) for n in range(2)]
            + [Step("stash", 1, b)] + to_qkv(1, b))


def post(b):
    return (project(1, b) + norm(1, b, 4) + [Step("quant", 1, b), Step("qt", 1, b)]
            + [Step("ffn", 1, b, n) for n in range(2)] + [Step("store", 1, b)])


def pack(layer, b):
    return [Step("pack", layer, b, g) for g in range(NG)]


def attention(layer, b):
    return [Step(o[0], layer, b, *o[1:]) for o in attention_order()]


def beside_own(att, other, packs):
    return beside(att, [s for s in other if s.kind != "v"], [s for s in other if s.kind == "v"] + packs, len(packs))


def beside(att, other, packs=(), n_packs=NG):
    steps, done, packed, through = [], 0, 0, 0
    span = FILL * len(att)
    for i, a in enumerate(att):
        while done < len(other) and done * span <= i * len(other):
            steps.append(other[done])
            done += 1
        steps.append(a)
        if a.kind == "chunk" and a.at[1] == NCH - 1:
            through += 1
        while done == len(other) and packed < min(through, len(packs)) and len(packs) == n_packs:
            steps.append(packs[packed])
            packed += 1
    return steps + list(other[done:]) + list(packs[packed:])


def number(layer, b):
    if layer == 0:
        return Affine(0, 0) if b.k == 0 and b.c == 0 else b.times(2) + -1
    return Affine(0, 2 * B - 1) if b.k == 0 and b.c == B - 1 else b.times(2) + 2


class Section:

    def __init__(self, steps):
        self.steps = []
        for s in steps:
            self.steps += [Step("w1", s.layer, s.sample, m) for m in range(4)] if s.kind == "experts" else [s]
        self.uses = {}
        for s in self.steps:
            if s.kind in SLOTTED:
                assert s.key not in self.uses
                self.uses[s.key] = len(self.uses)
        self.count = [(len(self.uses) + 1) // 2, len(self.uses) // 2]


def plan():
    def at(n):
        return Affine(0, n)

    def turn(i, n=None):
        return [Section(beside(attention(0, i), mid(i + -1), pack(1, i + -1))),
                Section(beside(attention(1, i + -1), ([] if n == 1 else post(i + -2)) + pre(i + 1), pack(0, i + 1)))]

    start = [Section(pre(at(0)) + pack(0, at(0))),
             Section(beside_own(attention(0, at(0)), pre(at(1)), pack(0, at(1))))] + turn(at(1), 1)
    loop = turn(Affine(1, 0))
    end = [Section(beside(attention(0, at(B - 1)), mid(at(B - 2)), pack(1, at(B - 2)))),
           Section(beside_own(attention(1, at(B - 2)), post(at(B - 3)) + mid(at(B - 1)), pack(1, at(B - 1)))),
           Section(beside(attention(1, at(B - 1)), post(at(B - 2)))),
           Section(post(at(B - 1)))]
    lo, hi = 2, B - 1
    before = [0, 0]
    for s in start:
        s.before = [Affine(0, n) for n in before]
        before = [n + c for n, c in zip(before, s.count)]
    per = [sum(s.count[j] for s in loop) for j in range(2)]
    at_turn = [Affine(per[j], before[j] - lo * per[j]) for j in range(2)]
    for s in loop:
        s.before = list(at_turn)
        at_turn = [a + c for a, c in zip(at_turn, s.count)]
    before = [n + (hi - lo) * p for n, p in zip(before, per)]
    for s in end:
        s.before = [Affine(0, n) for n in before]
        before = [n + c for n, c in zip(before, s.count)]
    return start, loop, end, lo, hi


START, LOOP, END, LO, HI = plan()


def tower(nc, x, W, b, Wqvk, Wo0, Wg, ln_scale, ln_bias, W1, b1, W2, b2, Wqkv, Wo1, rhs,
          ident, causal, cosines, sines, pick, out):
    ctx = ExitStack()
    with ctx:
        def sb(name, shape, dt=F32):
            return ctx.enter_context(nc.sbuf_tensor(name, shape, dt))

        def sem(name):
            return ctx.enter_context(nc.semaphore(name))

        stash = nc.dram_tensor("stash", (2, B, TB, NT, D), F32, kind="Internal").ap()
        spread = nc.dram_tensor("spread", (2, 2, 3, D, T), BF16, kind="Internal").ap()

        probs_raw = sb("probs", [128, RING * GH * CUT])
        probs = probs_raw[0:TB, :].rearrange("p (r n) -> p r n", n=CUT)
        early = [0]

        def early_weight(rows, *dims):
            n = int(np.prod(dims))
            v = probs_raw[0:rows, early[0]:early[0] + n]
            early[0] += n
            assert early[0] <= RING * GH * CUT
            letters = "abcd"[:len(dims)]
            sizes = {c: d for c, d in zip(letters, dims)}
            return v.rearrange(f"p ({' '.join(letters)}) -> p {' '.join(letters)}", **sizes) if len(dims) > 1 else v

        pickf = early_weight(32, 4, 128)
        maskf = early_weight(TB, TB)
        w_tok = early_weight(128, KC, 128)
        w_g = early_weight(E, D)
        lns = early_weight(E, 2, D)
        w_1 = early_weight(128, KC, E, HID)
        b_2 = early_weight(E, D)
        b_2r = early_weight(E, D)
        w_raw = early_weight(128, 6, D)
        rhs_t = early_weight(128, KC, D)

        identf = sb("identf", [128, 128])
        identb = sb("identb", [128, 128], BF16)
        maskb = sb("maskb", [TB, TB], BF16)
        cos_sb = sb("cos_sb", [TB, NT, DH])
        sin_sb = sb("sin_sb", [TB, NT, DH])
        pickb = sb("pickb", [32, 4, 128], BF16)
        decay = sb("decay", [128, 1])
        ones = sb("ones", [128, TB])
        neghalf = sb("neghalf", [TB, NT])
        rank = sb("rank", [TB, E])
        wt_tok = sb("wt_tok", [128, D])
        b_tok = sb("b_tok", [TB, D])
        w_qvk = sb("w_qvk", [128, KC, 3 * D])
        w_o0 = sb("w_o0", [128, KC, D])
        wt_g = sb("wt_g", [128, KC, E])
        lnt = sb("lnt", [128, 2, KC, E])
        w_1s = sb("w_1s", [128, KC, E * HID])
        b_1 = sb("b_1", [128, 4])
        b_1e = sb("b_1e", [128, 4])
        w_2 = sb("w_2", [128, 4, D])
        b_2s = sb("b_2s", [32, D], BF16)
        w_qkv = sb("w_qkv", [128, KC, 3 * D])
        w_o1t = sb("w_o1t", [128, KC, D])
        r_abs = sb("r_abs", [128, 3, KC])
        rq = sb("rq", [128, KC, D], BF16)
        r_scale = sb("r_scale", [TB, D])

        res = sb("res", [TB, NT, D])
        stats = sb("stats", [TB, NT, 6])
        mv = sb("mv", [TB, NT, 2])
        veps = sb("veps", [TB, NT])
        rstd = sb("rstd", [TB, NT])
        xn = sb("xn", [TB, NT, D])
        xh = sb("xh", [TB, NT, D])
        ao = [sb(f"ao{n}", [TB, NT, D]) for n in range(2)]
        xt = sb("xt", [128, KC, T])
        rest = sb("rest", [128, 2, T])
        xs, bwd = rest[:, 0, :], rest[:, 1, :]
        parts = sb("parts", [128, 2, 3, T], BF16)
        rq_t = parts[:, 0, 0, 0:2 * D].rearrange("p (c n) -> p c n", c=KC)
        b_2p = parts[0:E, 1, :, 0:D]
        qp = sb("qp", [SROWS, H, T], BF16)
        kp = sb("kp", [SROWS, H, T], BF16)
        va = [sb(f"va{n}", [TB, NT, H, DH + 1]) for n in range(2)]
        mx = sb("mx", [TB, 2, GH, NT])
        ms = sb("ms", [TB, 2, 3, GH * NT], BF16)
        mr = sb("mr", [TB, GH * NT])
        mt = sb("mt", [3 * GH * NT, 2, TB], BF16)
        os_ = sb("os", [128, T])
        rden = sb("rden", [TB, NT, GH])
        hidden = sb("hidden", [128, NT * 2 * D])
        ghid = hidden[:, 0:4 * T].rearrange("p (m t) -> p m t", m=4)
        qr = hidden[0:TB, :].rearrange("p (t n) -> p t n", t=NT)
        xin, fwd = hidden[:, 0:T], hidden[:, T:2 * T]
        w_o1 = hidden[:, 0:KC * D].rearrange("p (c n) -> p c n", c=KC)
        r_diag = hidden[:, KC * D:KC * (D + 128)].rearrange("p (c n) -> p c n", c=KC)
        qb = hidden[0:TB, 2 * T:2 * T + NT * D // 2].bitcast(BF16).rearrange("p (t n) -> p t n", t=NT)
        scratch = sb("scratch", [128, 4 * D])
        rot = scratch[0:TB, :].rearrange("p (a n) -> p a n", a=2)
        qbt = scratch[:, 0:KC * T // 2].bitcast(BF16).rearrange("p (c t) -> p c t", c=KC)
        lg = sb("lg", [TB, NT, E])
        lgm = sb("lgm", [TB, 2, NT])
        sel = sb("sel", [TB, NT, E])
        mk = sb("mk", [TB, NT, 32], BF16)
        mkt = sb("mkt", [32, NT, TB], BF16)
        am = sb("am", [TB, 3, NT])

        slot = [ctx.enter_context(nc.psum_tensor(f"slot{i}", [128, 2, 512], F32)) for i in range(2)]
        st = [ctx.enter_context(nc.psum_tensor(f"st{i}", [128, 512], F32)) for i in range(2)]
        acc = ctx.enter_context(nc.psum_tensor("acc", [128, 2, 512], F32))
        slotb = [s[:].bitcast(BF16) for s in slot]
        stb = [s[:].bitcast(BF16) for s in st]

        signals = []

        class Signal:

            def __init__(self, name, per):
                self.sem, self.per = sem(name), per
                signals.append(self)

        turn = {}
        stands_apart = []
        s_waited = sem("waited")

        def stand_apart(eng):
            eng.sem_inc(s_waited, 1)

        def wait_at(eng, signal, at):
            value = at.c + 1
            if at.k:
                eng.wait_ge(signal.sem, turn[eng] * at.k + value)
                if eng in stands_apart:
                    stand_apart(eng)
            else:
                eng.wait_ge(signal.sem, value)

        def need(eng, signal, sample, n):
            wait_at(eng, signal, sample.times(signal.per) + n)

        def cut_before(layer, b, other):
            if layer == other:
                return b
            if layer == 1:
                return b + 2 if b.k or b.c + 1 < B else b + 1
            return b + -1 if b.k or b.c > 0 else b

        full = [Signal(f"slot{i}_full", None) for i in range(2)]
        done = [Signal(f"slot{i}_done", None) for i in range(2)]
        s_weights = sem("weights_loaded")
        s_setup = {n: sem(f"setup_{n}") for n in ("pool", "act", "dve", "pe", "b2", "side")}
        s_x = Signal("x_loaded", 16)
        s_xs = Signal("x_scaled", 1)
        s_scan = Signal("scanned", 2)
        s_ends = Signal("scan_ends", 2)
        s_ewma = Signal("ewma_ready", 1)
        s_stashed = [Signal(f"stashed{n}", 16) for n in range(2)]
        s_fetched = [Signal(f"fetched{n}", 16) for n in range(2)]
        s_stats = [Signal(f"norm{n}_stats", 1) for n in range(5)]
        s_mv = [Signal(f"norm{n}_moments", 1) for n in range(5)]
        s_veps = [Signal(f"norm{n}_veps", 1) for n in range(5)]
        s_rstd = [Signal(f"norm{n}_rstd", 1) for n in range(5)]
        s_norm = [Signal(f"norm{n}_done", NT) for n in range(5)]
        s_high = [Signal(f"part_high{n}", 2 * KC) for n in range(2)]
        s_mid = [Signal(f"part_mid{n}", 2 * KC) for n in range(2)]
        s_low = [Signal(f"part_low{n}", 2 * KC) for n in range(2)]
        s_spread = [[Signal(f"spread{n}_{c}", 2 * 16) for c in range(KC)] for n in range(2)]
        s_packed = [Signal(f"packed{g}", 2 * NSTRIP * 16) for g in range(NG)]
        s_ms = Signal("shift_parts", NG * 4)
        s_mrow = [Signal(f"shift_row{i}", (NG // 2) * 16) for i in range(2)]
        s_scores = Signal("scores_ready", NG * NCH * GH)
        s_exp = Signal("exp_done", NG * NCH * GH)
        s_masked = Signal("masked", NG * NMASKED)
        s_pv = Signal("values_summed", NG * NCH)
        s_osb = Signal("sums_copied", NG)
        s_rden = Signal("denominators", NG)
        s_qr = Signal("rotary_done", NT)
        s_gate = Signal("gate_steps", 5)
        s_mk = Signal("gate_masks", 2)
        s_amax = Signal("quant_scale", 3)
        s_quant = Signal("quant_steps", NT + 2)
        s_out = Signal("result_ready", 1)
        s_stored = Signal("stored", 16)

        here = {}

        def await_done(eng, *keys, free=None, before=False):
            s = here[eng]
            at = {0: 0, 1: 0} if before else {}
            for k in [s.uses[key] for key in keys] + ([] if free is None else [s.uses[free] - 2]):
                at[k % 2] = max(at.get(k % 2, 0), k // 2 + 1)
            for i, n in at.items():
                wait_at(eng, done[i], s.before[i] + n)

        def take(eng, step, *results, before=False):
            await_done(eng, *results, free=step.key, before=before)
            return slot[here[eng].uses[step.key] % 2]

        def filled(eng, ins, step):
            ins.then_inc(full[here[eng].uses[step.key] % 2].sem, 1)

        def await_full(eng, key):
            s = here[eng]
            k = s.uses[key]
            wait_at(eng, full[k % 2], s.before[k % 2] + (k // 2 + 1))
            return slot[k % 2]

        def consumed(eng, ins, step):
            ins.then_inc(done[here[eng].uses[step.key] % 2].sem, 1)

        def low_view(eng, step):
            return slotb[here[eng].uses[step.key] % 2]

        def walk(eng, doing):
            def sections(those):
                for here[eng] in those:
                    for s in here[eng].steps:
                        if s.kind in doing:
                            doing[s.kind](s, s.layer, s.sample, *s.at)

            sections(START)
            with eng.Fori(LO, HI) as i:
                turn[eng] = i
                sections(LOOP)
            sections(END)

        weights = [
            (identf[:], ident), (maskf, causal),
            (cos_sb[:], cosines.rearrange("(t p) d -> p t d", p=TB)),
            (sin_sb[:], sines.rearrange("(t p) d -> p t d", p=TB)),
            (pickf, pick),
            (w_tok, W.rearrange("(c p) i -> p c i", p=128)),
            (b_tok[:], b.partition_broadcast(TB)),
            (w_qvk[:], Wqvk.rearrange("(c p) n -> p c n", p=128)),
            (w_o0[:], Wo0.rearrange("(c p) n -> p c n", p=128)),
            (w_g, Wg), (lns[:, 0, :], ln_scale), (lns[:, 1, :], ln_bias),
            (b_2, b2),
            (w_2[:], W2.rearrange("(c e) h n -> (e h) c n", e=2)),
            (w_raw, Wqkv.rearrange("(c p) n -> p c n", p=128)),
            (w_o1, Wo1.rearrange("(c p) n -> p c n", p=128)),
            (rhs_t, rhs.rearrange("(c p) n -> p c n", p=128)),
        ]
        for c in range(KC):
            weights.append((w_1[:, c], W1.rearrange("e (c p) h -> c p e h", p=128)[c]))
        for c in range(4):
            weights.append((b_1[:, c:c + 1], b1.rearrange("(c e) h -> c (e h)", e=2)[c].rearrange("(p a) -> p a", a=1)))
        n_weights = 16 * len(weights)

        block = ctx.enter_context(nc.Block())

        @block.sync
        def _(sp):
            def of_sample(dram, b):
                if b.k:
                    return dram[bass.ds(turn[sp] + b.c, 1)].rearrange("a p t d -> p (a t) d")
                return dram[b.c]

            def setup():
                for signal in signals:
                    sp.sem_inc(signal.sem, 1)
                for dst, src in weights:
                    sp.dma_start(dst, src).then_inc(s_weights, 16)
                sp.wait_ge(s_setup["dve"], 11)
                sp.wait_ge(s_setup["pool"], 5)
                for p in range(3):
                    sp.dma_start(b_2s[p * E:(p + 1) * E, :], b_2p[:, p, :]).then_inc(s_setup["b2"], 16)
                sp.wait_ge(s_setup["b2"], 48)
                sp.wait_ge(s_setup["pe"], 9)

            def scan(s, layer, b):
                await_done(sp, before=True)
                need(sp, s_ewma, b, 0)
                xv = x[bass.ds(turn[sp] + b.c, 1)].rearrange("a c t -> (a c) t") if b.k else x[b.c]
                sp.dma_start(xin, xv).then_inc(s_x.sem, 16)

            def stash_(s, layer, b):
                key = ("tok", 0, 2) if layer == 0 else ("w2", 0, 1)
                await_done(sp, key)
                sp.dma_start(of_sample(stash[layer], b), res[:]).then_inc(s_stashed[layer].sem, 16)

            def fetch(s, layer, b):
                need(sp, s_stashed[layer], b, 16)
                if layer == 0:
                    if b.k or b.c + 1 < B:
                        need(sp, s_stashed[0], b + 1, 16)
                    else:
                        need(sp, s_stored, b + -2, 16)
                else:
                    need(sp, s_stored, b, 0)
                    need(sp, s_stashed[1], *((b + 1, 16) if b.k or b.c + 1 < B else (b, 16)))
                sp.dma_start(res[:], of_sample(stash[layer], b)).then_inc(s_fetched[layer].sem, 16)

            def qk(s, layer, b, w, c):
                need(sp, s_low[layer], b, w * KC + c + 1)
                if w == 0 and c == 0 and (b.k or b.c > 0):
                    for g in range(NG):
                        need(sp, s_packed[g], number(layer, b + -1), 2 * NSTRIP * 16)
                sp.dma_start(spread[layer, w].rearrange("q (c p) t -> c p q t", c=KC)[c],
                             parts[:, c, :, :]).then_inc(s_spread[layer][c].sem, 16)

            def pack(s, layer, b, g):
                if g == 0:
                    for c in range(KC):
                        need(sp, s_spread[layer][c], b, 32)
                a = number(layer, b)
                if a.k or a.c > 0:
                    need(sp, s_scores, a + -1, (g + 1) * NCH * GH)
                for w in range(2):
                    for strip, part in enumerate((Q_PARTS, K_PARTS)[w]):
                        sp.dma_start((qp, kp)[w][strip * DH:(strip + 1) * DH, g * GH:(g + 1) * GH, :],
                                     spread[layer, w, part].rearrange("(h d) t -> d h t", d=DH)[:, g * GH:(g + 1) * GH, :])\
                            .then_inc(s_packed[g].sem, 16)

            def shift(s, layer, b, g):
                await_done(sp, s.key)
                sp.dma_start(qp[KROWS:SROWS, g * GH:(g + 1) * GH, :], mt[:, g % 2, :])\
                    .then_inc(s_mrow[g % 2].sem, 16)

            def store(s, layer, b):
                need(sp, s_out, b, 1)
                sp.dma_start(of_sample(out.rearrange("b (t p) d -> b p t d", p=TB), b), res[:]).then_inc(s_stored.sem, 16)

            setup()
            stands_apart.append(sp)
            walk(sp, {"scan": scan, "stash": stash_, "fetch": fetch, "qk": qk, "pack": pack, "shift": shift,
                      "store": store})
            sp.wait_ge(s_stored.sem, B * 16 + 1)

        @block.tensor
        def _(pe):
            mm = nc.tensor.matmul

            def setup():
                pe.wait_ge(s_weights, n_weights)
                pe.wait_ge(s_setup["pool"], 7)
                a = slot[0]
                for c in range(KC):
                    last = nc.tensor.transpose(a[:, 0, c * 128:(c + 1) * 128], w_tok[:, c, :], identf[:])
                last.then_inc(s_setup["pe"], 1)
                for c in range(KC):
                    cols = slice(c * 128, (c + 1) * 128)
                    nc.tensor.transpose(a[:, 1, c * 8:c * 8 + 8], w_g[:, cols], identf[0:E, 0:E])
                    for v in range(2):
                        o = 16 + v * 16 + c * 8
                        last = nc.tensor.transpose(a[:, 1, o:o + 8], lns[:, v, cols], identf[0:E, 0:E])
                last.then_inc(s_setup["pe"], 1)
                for c in range(KC):
                    s = slot[1]
                    if c:
                        pe.wait_ge(s_setup["act"], 3)
                    for r in range(6):
                        last = nc.tensor.transpose(s[:, r // 3, r % 3 * 128:r % 3 * 128 + 128],
                                                   w_raw[:, r, c * 128:(c + 1) * 128], identf[:])
                    last.then_inc(s_setup["pe"], 1)
                for c in range(KC):
                    for r in range(KC):
                        last = nc.tensor.transpose(st[0][:, (c * KC + r) * 128:(c * KC + r + 1) * 128],
                                                   w_o1[:, r, c * 128:(c + 1) * 128], identf[:])
                last.then_inc(s_setup["pe"], 1)
                for c in range(KC):
                    for r in range(KC):
                        last = nc.tensor.transpose(st[1][:, (c * KC + r) * 128:(c * KC + r + 1) * 128],
                                                   rhs_t[:, r, c * 128:(c + 1) * 128], identf[:])
                last.then_inc(s_setup["pe"], 1)
                pe.wait_ge(s_setup["act"], 2)
                pe.wait_ge(s_setup["dve"], 1)
                for e in range(E):
                    for c in range(KC):
                        last = mm(acc[64 * (e % 2):64 * (e % 2) + 64, 0, e // 2:e // 2 + 1],
                                  w_1[:, c, e, :], lnt[:, 1, c, e:e + 1], start=(c == 0), stop=(c == KC - 1))
                last.then_inc(s_setup["pe"], 1)
                pe.wait_ge(s_setup["dve"], 8)
                pe.wait_ge(s_setup["act"], 5)
                for c in range(KC):
                    for r in range(KC):
                        last = nc.tensor.transpose(stb[0][:, (c * KC + r) * 128:(c * KC + r + 1) * 128],
                                                   rq_t[:, r, c * 128:(c + 1) * 128], identb[:])
                last.then_inc(s_setup["pe"], 1)
                for c in range(KC):
                    last = mm(acc[0:TB, 1, c * 128:(c + 1) * 128], ones[:], r_diag[:, c, :], start=True, stop=True)
                last.then_inc(s_setup["pe"], 1)
                pe.wait_ge(s_setup["dve"], 12)
                pe.wait_ge(s_setup["act"], 8)
                pe.wait_ge(s_setup["b2"], 48)

            def turned(s, src, c, ready, results=(), before=False):
                o = take(pe, s, *results, before=before)
                for t in range(NT):
                    ready(t)
                    last = nc.tensor.transpose(o[:, t // 3, t % 3 * TB:t % 3 * TB + TB],
                                               src[:, t, c * 128:(c + 1) * 128], identf[0:TB, 0:TB])
                filled(pe, last, s)

            def by_blocks(s, after, n, lhs, rhs_of, nk, more=None):
                o = take(pe, s, *after)
                for j in range(3):
                    t = n * 3 + j
                    to = o[0:TB, j // 2, j % 2 * D:j % 2 * D + D]
                    for c in range(nk):
                        last = mm(to, lhs[:, c, t * TB:(t + 1) * TB], rhs_of(c), start=(c == 0),
                                  stop=(c == nk - 1 and more is None))
                    if more is not None:
                        last = mm(to, more[0][:, t, :], more[1], start=False, stop=True)
                filled(pe, last, s)

            def features_by(s, after, weight, extra=None):
                o = take(pe, s, *after)
                for half in range(2):
                    for c in range(KC):
                        last = mm(o[:, half, 0:HALF], weight(c), xt[:, c, half * HALF:(half + 1) * HALF],
                                  start=(c == 0), stop=(c == KC - 1 and extra is None))
                    if extra is not None:
                        last = mm(o[:, half, 0:HALF], extra,
                                  mkt[:, half * 3:half * 3 + 3, :].rearrange("p a b -> p (a b)"), start=False, stop=True)
                filled(pe, last, s)

            def both(kind, layer, *at):
                return [(kind, layer) + at + (c,) for c in range(KC)]

            late = {}

            def max_(s, layer, b, g, u):
                if u == 0:
                    need(pe, s_packed[g], number(layer, b), 2 * NSTRIP * 16)
                i, h0, nh = MAX_UNITS[u]
                o = take(pe, s)
                n = (i + 1) * TB
                for j in range(nh):
                    h = g * GH + h0 + j
                    q = qp[0:KROWS, h, i * TB:(i + 1) * TB]
                    if nh == 4:
                        per = 4 if i == 0 else 2
                        pieces = [(j // per, j % per * n, 0, n)]
                    elif nh == 2:
                        pieces = [(j, 0, 0, n)]
                    else:
                        w = -(-n // 2)
                        pieces = [(0, 0, 0, w), (1, 0, n - w, n)]
                    for bank, col, k0, k1 in pieces:
                        diag = k1 == n
                        last = mm(o[0:TB, bank, col:col + k1 - k0], q, kp[0:KROWS, h, k0:k1],
                                  start=True, stop=not diag, skip_group_check=True)
                        if diag:
                            at = col + n - TB - k0
                            last = mm(o[0:TB, bank, at:at + TB], identb[0:TB, 0:TB], maskb[:],
                                      start=False, stop=True, skip_group_check=True)
                filled(pe, last, s)

            def shift(s, layer, b, g):
                take(pe, s)
                need(pe, s_ms, number(layer, b), (g + 1) * 4)
                filled(pe, nc.tensor.transpose(low_view(pe, s)[0:3 * GH * NT, 0, 0:TB],
                                               ms[:, g % 2, :, :].rearrange("p a b -> p (a b)"),
                                               identb[0:TB, 0:TB]), s)

            def chunk(s, layer, b, g, c):
                a = number(layer, b)
                if c == 0:
                    need(pe, s_mrow[g % 2], a, (g // 2 + 1) * 16)
                for j in range(GH):
                    n = (g * NCH + c) * GH + j
                    h = g * GH + j
                    need(pe, s_exp, a, max(n - 1, 0))
                    for kb, q0, q1, col in CHUNKS[c]:
                        last = mm(st[n % 2][0:TB, col:col + q1 - q0], kp[:, h, kb * TB:(kb + 1) * TB],
                                  qp[:, h, q0:q1], start=True, stop=True, skip_group_check=True)
                    last.then_inc(s_scores.sem, 1)
                if late:
                    values(*late.pop("chunk"))
                late["chunk"] = (layer, a, g, c)

            def values(layer, a, g, c):
                n = g * NCH + c
                if DIAGONAL[c] is None:
                    need(pe, s_exp, a, (n + 1) * GH)
                else:
                    need(pe, s_masked, a, g * NMASKED + sum(d is not None for d in DIAGONAL[:c + 1]) * GH)
                if c == 0:
                    need(pe, s_osb, a, g)
                for kb, q0, q1, col in CHUNKS[c]:
                    for f, z in ((q0, min(q1, CUT)), (max(q0, CUT), q1)):
                        if f >= z:
                            continue
                        bank = int(f >= CUT)
                        for j in range(GH):
                            ring = n % RING * GH + j
                            last = mm(acc[32 * j:32 * j + DH + 1, bank, f - CUT * bank:z - CUT * bank],
                                      va[layer][:, kb, g * GH + j, :],
                                      probs[:, ring, col + f - q0:col + z - q0],
                                      start=(kb == 0), stop=False, skip_group_check=True)
                last.then_inc(s_pv.sem, 1)

            def last_(s, layer, b, g):
                values(*late.pop("chunk"))

            def turn_(s, layer, b, g):
                o = take(pe, s)
                need(pe, s_osb, number(layer, b), g + 1)
                for t in range(NT):
                    last = nc.tensor.transpose(o[0:TB, t // 3, t % 3 * 128:t % 3 * 128 + 128],
                                               os_[:, t * TB:(t + 1) * TB], identf[:])
                filled(pe, last, s)

            def tok(s, layer, b, n):
                o = take(pe, s)
                need(pe, s_ewma, b, 1)
                for j in range(2):
                    t = n * 2 + j
                    last = mm(o[0:TB, j, 0:D], fwd[:, t * TB:(t + 1) * TB], wt_tok[:], start=True, stop=True)
                filled(pe, last, s)

            def xt_(s, layer, b, n, c):
                turned(s, xh if n == 2 else xn, c, lambda t: need(pe, s_norm[n], b, t + 1) if c == 0 else None)

            def qk(s, layer, b, w, c):
                if layer == 0:
                    col = w * 2 * D + c * 128
                    features_by(s, both("xt", 0, 0), lambda k: w_qvk[:, k, col:col + 128])
                else:
                    turned(s, qr[:, :, w * D:(w + 1) * D], c,
                           lambda t: need(pe, s_qr, b, t + 1) if w == 0 and c == 0 else None)

            def v(s, layer, b, n):
                w, col = ((w_qvk, D), (w_qkv, 2 * D))[layer]
                by_blocks(s, both("xt", layer, 3 * layer), n, xt, lambda c: w[:, c, col:col + D], KC)

            def ao_(s, layer, b, c):
                turned(s, ao[layer], c, lambda t: None, before=True)

            def wo(s, layer, b, n):
                w = (w_o0, w_o1t)[layer]
                by_blocks(s, both("ao", layer), n, xt, lambda c: w[:, c, :], KC)

            def logit(s, layer, b):
                o = take(pe, s, *both("xt", 0, 1))
                for t in range(NT):
                    for c in range(KC):
                        last = mm(o[0:TB, 0, t * E:(t + 1) * E], xt[:, c, t * TB:(t + 1) * TB], wt_g[:, c, :],
                                  start=(c == 0), stop=(c == KC - 1))
                filled(pe, last, s)

            def mask(s, layer, b):
                take(pe, s)
                need(pe, s_mk, b, 2)
                for t in range(NT):
                    last = nc.tensor.transpose(low_view(pe, s)[0:32, 0, t * 128:t * 128 + TB],
                                               mk[:, t, :], identb[0:TB, 0:TB])
                filled(pe, last, s)

            def w1(s, layer, b, m):
                features_by(s, [("mask", 0)] + both("xt", 0, 2), lambda k: w_1s[:, k, m * 128:(m + 1) * 128],
                            pickb[:, m, :])

            def w2(s, layer, b, n):
                by_blocks(s, [("w1", 0, m) for m in range(4)], n, ghid, lambda c: w_2[:, c, :], 4, (mkt, b_2s[:]))

            def qktok(s, layer, b, n):
                o = take(pe, s, *both("xt", 1, 3))
                for j in range(2):
                    t = n * 2 + j
                    for c in range(KC):
                        last = mm(o[0:TB, j, :], xt[:, c, t * TB:(t + 1) * TB], w_qkv[:, c, 0:2 * D],
                                  start=(c == 0), stop=(c == KC - 1))
                filled(pe, last, s)

            def qt(s, layer, b):
                take(pe, s)
                need(pe, s_quant, b, NT + 2)
                for c in range(KC):
                    for t in range(NT):
                        last = nc.tensor.transpose(low_view(pe, s)[:, c, t * 128:t * 128 + TB],
                                                   qb[:, t, c * 128:(c + 1) * 128], identb[0:TB, 0:TB])
                filled(pe, last, s)

            def ffn(s, layer, b, n):
                by_blocks(s, [("qt", 1)], n, qbt, lambda c: rq[:, c, :], KC)

            setup()
            walk(pe, {"max": max_, "shift": shift, "chunk": chunk, "last": last_, "turn": turn_, "tok": tok, "xt": xt_,
                      "qk": qk, "v": v, "ao": ao_, "wo": wo, "logit": logit, "mask": mask, "w1": w1, "w2": w2,
                      "qktok": qktok, "qt": qt, "ffn": ffn})

        @block.scalar
        def _(act):
            def copy(o, i):
                return nc.scalar.activation(o, i, ACT.Copy)

            def setup():
                act.wait_ge(s_setup["pe"], 1)
                nc.scalar.mul(wt_tok[:], slot[0][:, 0, 0:D], 0.5).then_inc(s_setup["act"], 1)
                act.wait_ge(s_setup["pe"], 2)
                copy(wt_g[:].rearrange("p c e -> p (c e)"), slot[0][:, 1, 0:16])
                copy(lnt[:].rearrange("p a c e -> p (a c e)"), slot[0][:, 1, 16:48]).then_inc(s_setup["act"], 1)
                for c in range(KC):
                    act.wait_ge(s_setup["pe"], 3 + c)
                    copy(w_qkv[:, c, :].rearrange("p (a n) -> p a n", a=2), slot[1][:, :, 0:384])\
                        .then_inc(s_setup["act"], 1)
                act.wait_ge(s_setup["pe"], 5)
                copy(w_o1t[:].rearrange("p c n -> p (c n)"), st[0][:]).then_inc(s_setup["act"], 1)
                act.wait_ge(s_setup["pe"], 7)
                copy(b_1e[:], acc[:, 0, 0:4]).then_inc(s_setup["act"], 1)
                act.wait_ge(s_setup["pe"], 8)
                copy(rq[:].rearrange("p c n -> p (c n)"), stb[0][:, 0:2 * D]).then_inc(s_setup["act"], 1)
                act.wait_ge(s_setup["pe"], 9)
                copy(r_scale[:], acc[0:TB, 1, 0:D]).then_inc(s_setup["act"], 1)

            def scan(s, layer, b):
                need(act, s_x, b, 16)
                need(act, s_scan, b, 2)
                copy(fwd[:, 0:1], xin[:, 0:1]).then_inc(s_ends.sem, 1)
                copy(bwd[:, T - 1:T], xin[:, T - 1:T]).then_inc(s_ends.sem, 1)

            def copy_turned(s, c):
                o = await_full(act, s.key)
                consumed(act, copy(xt[:, c, :].rearrange("p (a n) -> p a n", a=2), o[:, :, 0:HALF]), s)

            def v(s, layer, b, n):
                o = await_full(act, s.key)
                to = va[layer]
                copy(to[:, n * 3:n * 3 + 2, :, 0:DH], o[0:TB, 0, :].rearrange("p (t h d) -> p t h d", t=2, h=H))
                consumed(act, copy(to[:, n * 3 + 2, :, 0:DH], o[0:TB, 1, 0:D].rearrange("p (h d) -> p h d", h=H)), s)

            def qk(s, layer, b, w, c):
                o = await_full(act, s.key)
                if w == 0:
                    for other in range(2):
                        need(act, s_spread[other][c], cut_before(layer, b, other), 0)
                else:
                    need(act, s_spread[layer][c], b, 16)
                copy(parts[:, c, 0, :].rearrange("p (a n) -> p a n", a=2), o[:, :, 0:HALF]).then_inc(s_high[layer].sem, 1)

            def shift(s, layer, b, g):
                await_full(act, s.key)
                need(act, s_mrow[g % 2], number(layer, b), g // 2 * 16)
                consumed(act, copy(mt[:, g % 2, :], low_view(act, s)[0:3 * GH * NT, 0, 0:TB]), s)

            def chunk(s, layer, b, g, c):
                scale = (1.0 / 16.0, 0.25)[layer]
                a = number(layer, b)
                k = g * NCH + c
                for j in range(GH):
                    n = k * GH + j
                    need(act, s_scores, a, n + 1)
                    need(act, s_pv, a, max(k - RING + 1, 0))
                    nc.scalar.activation(probs[:, k % RING * GH + j, 0:WIDTH[c]], st[n % 2][0:TB, 0:WIDTH[c]],
                                         ACT.Exp, scale=scale).then_inc(s_exp.sem, 1)
                if c == 0 and g > 0:
                    copy_sums(s, layer, a, g - 1)

            def copy_sums(s, layer, a, g):
                need(act, s_pv, a, (g + 1) * NCH)
                if g > 0:
                    await_full(act, ("turn", layer, g - 1))
                copy(os_[:, 0:CUT], acc[:, 0, 0:CUT])
                copy(os_[:, CUT:T], acc[:, 1, 0:T - CUT]).then_inc(s_osb.sem, 1)

            def last_(s, layer, b, g):
                copy_sums(s, layer, number(layer, b), g)

            def mask(s, layer, b):
                await_full(act, s.key)
                rows = low_view(act, s)[0:32, 0, 0:NT * 128].rearrange("p (t n) -> p t n", t=NT)
                consumed(act, copy(mkt[:], rows[:, :, 0:TB]), s)

            def w1(s, layer, b, m):
                o = await_full(act, s.key)
                consumed(act, nc.scalar.activation(ghid[:, m, :].rearrange("p (a n) -> p a n", a=2), o[:, :, 0:HALF],
                                                   ACT.Gelu, bias=b_1[:, m:m + 1]), s)

            def qt(s, layer, b):
                await_full(act, s.key)
                rows = low_view(act, s)[:, :, 0:NT * 128].rearrange("p c (t n) -> p c t n", t=NT)
                consumed(act, copy(qbt.rearrange("p c (t n) -> p c t n", t=NT), rows[:, :, :, 0:TB]), s)

            setup()
            walk(act, {"scan": scan, "xt": lambda s, layer, b, n, c: copy_turned(s, c),
                       "ao": lambda s, layer, b, c: copy_turned(s, c), "v": v, "qk": qk, "shift": shift,
                       "chunk": chunk, "last": last_, "mask": mask, "w1": w1, "qt": qt})

        @block.gpsimd
        def _(pool):
            def setup():
                g = nc.gpsimd
                g.memset(decay[:], 1.0 - ALPHA).then_inc(s_setup["pool"], 1)
                g.memset(ones[:], 1.0).then_inc(s_setup["pool"], 1)
                g.memset(neghalf[:], -0.5).then_inc(s_setup["pool"], 1)
                for layer in range(2):
                    last = g.memset(va[layer][:], 1.0)
                last.then_inc(s_setup["pool"], 1)
                g.memset(b_2s[:], 0.0).then_inc(s_setup["pool"], 1)
                for e in range(E):
                    last = g.memset(rank[:, e:e + 1], float(E - e))
                last.then_inc(s_setup["pool"], 1)
                g.memset(rden[:], 0.0).then_inc(s_setup["pool"], 1)

            def stats_(s, layer, b, n):
                need(pool, s_mv[n], b, 1)
                nc.gpsimd.tensor_scalar(veps[:], mv[:, :, 1], EPS, None, ALU.add).then_inc(s_veps[n].sem, 1)
                need(pool, s_veps[n], b, 1)
                nc.gpsimd.tensor_tensor(rstd[:], veps[:], neghalf[:], ALU.pow).then_inc(s_rstd[n].sem, 1)

            def qk(s, layer, b, w, c):
                need(pool, s_mid[layer], b, w * KC + c + 1)
                nc.gpsimd.tensor_tensor(parts[:, c, 2, :], rest[:, c, :], parts[:, c, 1, :],
                                        ALU.subtract).then_inc(s_low[layer].sem, 1)

            def chunk(s, layer, b, g, c):
                if DIAGONAL[c] is None:
                    return
                k = g * NCH + c
                for j in range(GH):
                    need(pool, s_exp, number(layer, b), k * GH + j + 1)
                    p = probs[:, k % RING * GH + j, :]
                    if c == 2:
                        o, pattern = p[:, 0:500].rearrange("p (a n) -> p a n", a=4)[:, 0::3, :], [[0, 2], [1, TB]]
                    else:
                        o, pattern = p[:, 0:TB], [[1, TB]]
                    nc.gpsimd.affine_select(out=o, in_=o, compare_op=ALU.is_ge, fill=0.0, base=0,
                                            pattern=pattern, channel_multiplier=-1).then_inc(s_masked.sem, 1)

            def qktok(s, layer, b, n):
                await_done(pool, s.key)
                for j in range(2):
                    t = 2 * n + j
                    nc.gpsimd.tensor_tensor(qr[:, t, :], qr[:, t, :], rot[:, j, :], ALU.add).then_inc(s_qr.sem, 1)

            setup()
            stands_apart.append(pool)
            walk(pool, {"stats": stats_, "qk": qk, "chunk": chunk, "qktok": qktok})

        @block.vector
        def _(dve):
            v = nc.vector

            def setup():
                n, side = s_setup["dve"], s_setup["side"]
                v.memset(acc[:], 0.0).then_inc(n, 1)
                dve.wait_ge(s_weights, n_weights)
                v.tensor_copy(identb[:], identf[:])
                v.tensor_copy(maskb[:], maskf).then_inc(n, 1)
                v.memset(kp[KROWS:SROWS, :, :], 1.0)
                v.tensor_copy(pickb[:], pickf).then_inc(n, 1)
                dve.wait_ge(s_setup["pe"], 6)
                src = st[1][:].rearrange("p (c n) -> p c n", c=KC)
                v.tensor_reduce(r_abs[:, 0, :], src, AX.X, ALU.max, apply_absolute_value=True).then_inc(n, 1)
                dve.wait_ge(n, 4)
                v.tensor_scalar(r_abs[:, 1, :], r_abs[:, 0, :], 1e-12, 1.0 / INT8_MAX, ALU.max, ALU.mult).then_inc(n, 1)
                dve.wait_ge(n, 5)
                v.reciprocal(r_abs[:, 2, :], r_abs[:, 1, :]).then_inc(n, 1)
                dve.wait_ge(n, 6)
                for c in range(KC):
                    v.tensor_scalar(rhs_t[:, c, :], src[:, c, :], r_abs[:, 2, c:c + 1], INT8_MAX, ALU.mult, ALU.min)
                    last = v.tensor_scalar(r_diag[:, c, :], identf[:], r_abs[:, 1, c:c + 1], None, ALU.mult)
                last.then_inc(n, 1)
                dve.wait_ge(n, 7)
                v.tensor_scalar(rhs_t, rhs_t, -INT8_MAX, MAGIC, ALU.max, ALU.add).then_inc(side, 1)
                dve.wait_ge(side, 1)
                v.tensor_scalar(rq_t, rhs_t, MAGIC, None, ALU.subtract).then_inc(n, 1)
                v.tensor_copy(b_2p[:, 0, :], b_2).then_inc(side, 1)
                dve.wait_ge(side, 2)
                v.tensor_tensor(b_2r, b_2, b_2p[:, 0, :], ALU.subtract).then_inc(n, 1)
                dve.wait_ge(n, 9)
                v.tensor_copy(b_2p[:, 1, :], b_2r).then_inc(n, 1)
                dve.wait_ge(n, 10)
                v.tensor_tensor(b_2p[:, 2, :], b_2r, b_2p[:, 1, :], ALU.subtract).then_inc(n, 1)
                dve.wait_ge(s_setup["act"], 6)
                for c in range(KC):
                    for e in range(E):
                        v.tensor_scalar(w_1s[:, c, e * HID:(e + 1) * HID], w_1[:, c, e, :],
                                        lnt[:, 0, c, e:e + 1], None, ALU.mult)
                v.tensor_tensor(b_1[:], b_1[:], b_1e[:], ALU.add).then_inc(n, 1)
                dve.wait_ge(s_setup["act"], 8)
                dve.wait_ge(s_setup["pool"], 7)

            def scan(s, layer, b):
                need(dve, s_x, b, 16)
                for other in range(2):
                    need(dve, s_low[other], cut_before(0, b, other), 0)
                v.tensor_scalar(xs, xin, ALPHA, None, ALU.mult).then_inc(s_xs.sem, 1)
                need(dve, s_xs, b, 1)
                factor = decay[:].broadcast_to([128, T - 1])
                v.tensor_tensor_scan(fwd[:, 1:T], factor, xs[:, 1:T], xin[:, 0:1],
                                     ALU.mult, ALU.add).then_inc(s_scan.sem, 1)
                v.tensor_tensor_scan(bwd[:, 0:T - 1][:, ::-1], factor, xs[:, 0:T - 1][:, ::-1],
                                     xin[:, T - 1:T], ALU.mult, ALU.add).then_inc(s_scan.sem, 1)
                need(dve, s_scan, b, 2)
                need(dve, s_ends, b, 2)
                v.tensor_tensor(fwd, fwd, bwd, ALU.add).then_inc(s_ewma.sem, 1)

            def tok(s, layer, b, n):
                o = await_full(dve, s.key)
                if n == 0:
                    if b.k or b.c > 2:
                        need(dve, s_stored, b + -3, 16)
                    if b.k or b.c > 1:
                        need(dve, s_stashed[1], b + -2, 16)
                    need(dve, s_stashed[0], b, 0)
                consumed(dve, v.tensor_tensor(res[:, 2 * n:2 * n + 2, :], o[0:TB, :, 0:D],
                                              b_tok[:].unsqueeze(1).broadcast_to([TB, 2, D]), ALU.add), s)

            def source(n):
                return (xn if n == 2 else res), (xh if n == 2 else xn)

            def stats_(s, layer, b, n):
                src, _ = source(n)
                if n == 0:
                    await_done(dve, ("tok", 0, 2))
                elif n == 3:
                    await_done(dve, ("w2", 0, 1))
                elif n != 2:
                    await_done(dve, ("wo", layer, 1))
                for t in range(NT):
                    if n == 2:
                        need(dve, s_norm[1], b, t + 1)
                    last = v.bn_stats(stats[:, t, :], src[:, t, :])
                last.then_inc(s_stats[n].sem, 1)
                need(dve, s_stats[n], b, 1)
                stand_apart(dve)
                for t in range(NT):
                    last = v.bn_aggr(mv[:, t, :], stats[:, t, :])
                last.then_inc(s_mv[n].sem, 1)

            def apply(s, layer, b, n):
                src, dst = source(n)
                need(dve, s_rstd[n], b, 1)
                for t in range(NT):
                    v.tensor_scalar(dst[:, t, :], src[:, t, :], mv[:, t, 0:1], rstd[:, t:t + 1],
                                    ALU.subtract, ALU.mult).then_inc(s_norm[n].sem, 1)

            def add_to_res(s, n):
                o = await_full(dve, s.key)
                a, z = res[:, n * 3:n * 3 + 2, :], res[:, n * 3 + 2, :]
                v.tensor_tensor(a, o[0:TB, 0, :].rearrange("p (t d) -> p t d", t=2), a, ALU.add)
                consumed(dve, v.tensor_tensor(z, o[0:TB, 1, 0:D], z, ALU.add), s)

            def wo(s, layer, b, n):
                need(dve, s_fetched[layer], b, 16)
                add_to_res(s, n)

            def qk(s, layer, b, w, c):
                o = await_full(dve, s.key)
                need(dve, s_high[layer], b, w * KC + c + 1)
                if w == 1:
                    need(dve, s_low[layer], b, c + 1)
                else:
                    for other in range(2):
                        need(dve, s_low[other], cut_before(layer, b, other), 0)
                two = "p (a n) -> p a n"
                consumed(dve, v.tensor_tensor(rest[:, c, :].rearrange(two, a=2), o[:, :, 0:HALF],
                                              parts[:, c, 0, :].rearrange(two, a=2), ALU.subtract), s)
                await_done(dve, s.key)
                v.tensor_copy(parts[:, c, 1, :], rest[:, c, :]).then_inc(s_mid[layer].sem, 1)

            def max_(s, layer, b, g, u):
                i, h0, nh = MAX_UNITS[u]
                o = await_full(dve, s.key)
                n = (i + 1) * TB
                if i == 0:
                    src = o[0:TB, 0, 0:4 * n].rearrange("p (h t) -> p h t", h=4)
                elif i == 1:
                    src = o[0:TB, :, 0:2 * n].rearrange("p b (h t) -> p b h t", h=2)
                else:
                    src = o[0:TB, :, 0:(n if nh == 2 else -(-n // 2))]
                consumed(dve, v.tensor_reduce(mx[:, g % 2, h0:h0 + nh, i], src,
                                              AX.XY if nh == 1 else AX.X, ALU.max), s)
                if u == len(MAX_UNITS) - 1:
                    split_maxima(s, layer, number(layer, b), g)

            def split_maxima(s, layer, a, g):
                await_done(dve, s.key)
                m = mx[:, g % 2].rearrange("p h i -> p (h i)")
                v.tensor_scalar(ms[:, g % 2, 0, :], m, -1.0, None, ALU.mult).then_inc(s_ms.sem, 1)
                need(dve, s_ms, a, g * 4 + 1)
                v.scalar_tensor_tensor(out=mr[:], in0=m, scalar=-1.0, in1=ms[:, g % 2, 0, :],
                                       op0=ALU.mult, op1=ALU.subtract).then_inc(s_ms.sem, 1)
                need(dve, s_ms, a, g * 4 + 2)
                v.tensor_copy(ms[:, g % 2, 1, :], mr[:]).then_inc(s_ms.sem, 1)
                need(dve, s_ms, a, g * 4 + 3)
                v.tensor_tensor(ms[:, g % 2, 2, :], mr[:], ms[:, g % 2, 1, :], ALU.subtract).then_inc(s_ms.sem, 1)

            def turn_(s, layer, b, g):
                o = await_full(dve, s.key)
                if g > 0:
                    await_done(dve, ("turn", layer, g - 1))
                ov = o[0:TB, :, 0:384].rearrange("p b (t h f) -> p b t h f", t=3, h=GH)
                for bk in range(2):
                    last = v.reciprocal(rden[:, 3 * bk:3 * bk + 3, :], ov[:, bk, :, :, DH])
                last.then_inc(s_rden.sem, 1)
                need(dve, s_rden, number(layer, b), g + 1)
                for bk in range(2):
                    last = v.tensor_tensor(
                        ao[layer][:, 3 * bk:3 * bk + 3, g * 64:(g + 1) * 64].rearrange("p t (h d) -> p t h d", h=GH),
                        ov[:, bk, :, :, 0:DH],
                        rden[:, 3 * bk:3 * bk + 3, :].unsqueeze(3).broadcast_to([TB, 3, GH, DH]), ALU.mult)
                consumed(dve, last, s)

            def logit(s, layer, b):
                o = await_full(dve, s.key)
                consumed(dve, v.tensor_copy(lg[:], o[0:TB, 0, 0:NT * E].rearrange("p (t e) -> p t e", t=NT)), s)

            def gate(s, layer, b):
                await_done(dve, ("logit", 0))
                v.tensor_reduce(lgm[:, 0, :], lg[:], AX.X, ALU.max).then_inc(s_gate.sem, 1)
                need(dve, s_gate, b, 1)
                v.tensor_tensor(sel[:], lg[:], lgm[:, 0, :].unsqueeze(2).broadcast_to([TB, NT, E]), ALU.is_equal)\
                    .then_inc(s_gate.sem, 1)
                need(dve, s_gate, b, 2)
                v.tensor_tensor(sel[:], sel[:], rank[:].unsqueeze(1).broadcast_to([TB, NT, E]), ALU.mult)\
                    .then_inc(s_gate.sem, 1)
                need(dve, s_gate, b, 3)
                v.tensor_reduce(lgm[:, 1, :], sel[:], AX.X, ALU.max).then_inc(s_gate.sem, 1)
                need(dve, s_gate, b, 4)
                v.tensor_tensor(sel[:], sel[:], lgm[:, 1, :].unsqueeze(2).broadcast_to([TB, NT, E]), ALU.is_equal)\
                    .then_inc(s_gate.sem, 1)
                need(dve, s_gate, b, 5)
                for r in range(3):
                    last = v.tensor_copy(mk[:, :, r * E:(r + 1) * E], sel[:])
                last.then_inc(s_mk.sem, 1)
                v.tensor_scalar(mk[:, :, 3 * E:4 * E], sel[:], -NEG, NEG, ALU.mult, ALU.add).then_inc(s_mk.sem, 1)

            def qktok(s, layer, b, n):
                o = await_full(dve, s.key)
                need(dve, s_qr, b, 2 * n)
                for j in range(2):
                    t = 2 * n + j
                    v.tensor_tensor(qr[:, t, :].rearrange("p (h d) -> p h d", d=DH),
                                    o[0:TB, j, :].rearrange("p (h d) -> p h d", d=DH),
                                    cos_sb[:, t, :].unsqueeze(1).broadcast_to([TB, 2 * H, DH]), ALU.mult)
                    pairs = "p (h f two) -> p h f two"
                    last = v.tensor_tensor(
                        rot[:, j, :].rearrange(pairs, f=DH // 2, two=2),
                        o[0:TB, j, :].rearrange(pairs, f=DH // 2, two=2)[:, :, :, ::-1],
                        sin_sb[:, t, :].rearrange("p (f two) -> p f two", two=2).unsqueeze(1)
                        .broadcast_to([TB, 2 * H, DH // 2, 2]), ALU.mult)
                consumed(dve, last, s)

            def quant(s, layer, b):
                need(dve, s_norm[4], b, NT)
                v.tensor_reduce(am[:, 0, :], xn[:], AX.X, ALU.max, apply_absolute_value=True).then_inc(s_amax.sem, 1)
                need(dve, s_amax, b, 1)
                v.tensor_scalar(am[:, 1, :], am[:, 0, :], 1e-12, 1.0 / INT8_MAX, ALU.max, ALU.mult).then_inc(s_amax.sem, 1)
                need(dve, s_amax, b, 2)
                v.reciprocal(am[:, 2, :], am[:, 1, :]).then_inc(s_amax.sem, 1)
                need(dve, s_amax, b, 3)
                for t in range(NT):
                    v.tensor_scalar(xh[:, t, :], xn[:, t, :], am[:, 2, t:t + 1], INT8_MAX, ALU.mult, ALU.min)\
                        .then_inc(s_quant.sem, 1)
                need(dve, s_quant, b, NT)
                v.tensor_scalar(xh[:], xh[:], -INT8_MAX, MAGIC, ALU.max, ALU.add).then_inc(s_quant.sem, 1)
                need(dve, s_quant, b, NT + 1)
                v.tensor_scalar(qb, xh[:], MAGIC, None, ALU.subtract).then_inc(s_quant.sem, 1)

            def ffn(s, layer, b, n):
                o = await_full(dve, s.key)
                for j in range(3):
                    t = n * 3 + j
                    last = v.scalar_tensor_tensor(out=xh[:, t, :], in0=o[0:TB, j // 2, j % 2 * D:j % 2 * D + D],
                                                  scalar=am[:, 1, t:t + 1], in1=r_scale[:],
                                                  op0=ALU.mult, op1=ALU.mult)
                consumed(dve, last, s)

            def store(s, layer, b):
                await_done(dve, ("ffn", 1, 1), ("ffn", 1, 0))
                v.tensor_tensor(res[:], res[:], xh[:], ALU.add).then_inc(s_out.sem, 1)

            setup()
            walk(dve, {"scan": scan, "tok": tok, "stats": stats_, "apply": apply, "wo": wo,
                       "w2": lambda s, layer, b, n: add_to_res(s, n), "qk": qk, "max": max_, "turn": turn_,
                       "logit": logit, "gate": gate, "qktok": qktok, "quant": quant, "ffn": ffn, "store": store})


_IN = ['x', 'L0_tok_W', 'L0_tok_b', 'L0_attn_Wqvk', 'L0_attn_Wo', 'L0_ffn_Wg', 'L0_ffn_ln_scale', 'L0_ffn_ln_bias',
       'L0_ffn_W1', 'L0_ffn_b1', 'L0_ffn_W2', 'L0_ffn_b2', 'L1_attn_Wqkv', 'L1_attn_Wo', 'L1_ffn_rhs']


def _tables():
    pos = np.arange(T, dtype=np.float32)
    freqs = np.exp(np.float32(-np.log(10000.0)) * np.arange(0, DH, 2, dtype=np.float32) / np.float32(DH))
    angles = np.repeat(pos[:, None] * freqs.astype(np.float32)[None, :], 2, axis=-1)
    sign = np.tile(np.array([-1.0, 1.0], np.float32), DH // 2)
    causal = np.where(np.arange(TB)[None, :] > np.arange(TB)[:, None], np.float32(NEG), np.float32(0.0))
    pick = np.zeros((32, 4, 128), np.float32)
    for e in range(E):
        pick[3 * E + e, e // 2, e % 2 * HID:(e % 2 + 1) * HID] = 1.0
    return {
        "ident": np.eye(128, dtype=np.float32), "causal": causal.astype(np.float32),
        "cosines": np.cos(angles).astype(np.float32), "sines": (np.sin(angles) * sign).astype(np.float32),
        "pick": pick,
    }


def kernel(**inputs):
    import concourse.bacc as _bacc
    from concourse.bass_utils import run_bass_kernel_spmd as _run

    nc = _bacc.Bacc("TRN2", target_bir_lowering=False, num_devices=1)
    arrays = {f"in_{n}": np.ascontiguousarray(inputs[n]) for n in _IN}
    arrays |= {f"table_{n}": a for n, a in _tables().items()}
    args = [nc.dram_tensor(n, a.shape, mybir.dt.from_np(a.dtype), kind="ExternalInput").ap() for n, a in arrays.items()]
    out = nc.dram_tensor("out", (B, T, D), F32, kind="ExternalOutput").ap()
    tower(nc, *args, out)
    r = _run(nc, [arrays], core_ids=[0])
    return r.results[0]["out"]
```

```python
from contextlib import ExitStack

import numpy as np

import concourse.bass as bass
from concourse import mybir

F32 = mybir.dt.float32
BF16 = mybir.dt.bfloat16
ALU = mybir.AluOpType
ACT = mybir.ActivationFunctionType
AX = mybir.AxisListType

B, C_IN, T = 8, 128, 750
D, H, DH = 256, 16, 16
E, HID = 8, 64
TB = 125
NT = T // TB
HALF = T // 2
KC = D // 128
GH = 4
NG = H // GH
HPC = 128 // DH
ALPHA = 0.1
EPS = 1e-5
MAGIC = 1.5 * 2.0 ** 23
INT8_MAX = 127.0
NEG = -1e30
Q_PARTS = (0, 0, 1, 1, 0, 2)
K_PARTS = (0, 1, 0, 1, 2, 0)
NSTRIP = len(Q_PARTS)
KROWS = NSTRIP * DH
SROWS = KROWS + 3

MAX_UNITS = [(0, 0, 4, 0, TB), (1, 0, 2, 0, 2 * TB), (1, 2, 2, 0, 2 * TB)]
for _i in range(2, NT):
    _n = (_i + 1) * TB
    for _h in range(GH):
        _pieces = 1 if _n <= 512 else 2
        _w = -(-_n // _pieces)
        MAX_UNITS += [(_i, _h, 1, k0, _w) for k0 in (0, _n - _w)[:_pieces]]
SPLIT = 512 // TB
CHUNKS = [
    [(0, 0, 500, 0)],
    [(0, 500, 750, 0), (1, 500, 750, 250)],
    [(1, 125, 500, 0), (5, 625, 750, 375)],
    [(2, 250, 750, 0)],
    [(3, 375, 750, 0)],
    [(4, 500, 750, 0)],
]
NCH = len(CHUNKS)
WIDTH = [sum(q1 - q0 for _, q0, q1, _ in ch) for ch in CHUNKS]
DIAGONAL = [0, None, (0, 375), 0, 0, 0]
NMASKED = sum(d is not None for d in DIAGONAL) * GH
CUT = 500
RING = 3
LEAD = 12
STAGE_ENDS = 0.5

BESIDE_W1 = 2
SLOTS = 4
SLOTTED = ("max", "shift", "turn", "tok", "xt", "qk", "v", "ao", "wo", "logit", "mask", "w1", "w2", "qktok", "qt", "ffn")


class Affine:

    def __init__(self, k, c):
        self.k, self.c = k, c

    def __add__(self, n):
        return Affine(self.k, self.c + n)

    def times(self, n):
        return Affine(self.k * n, self.c * n)


class Step:
    def __init__(self, kind, layer, sample, *at):
        self.kind, self.layer, self.sample, self.at = kind, layer, sample, at
        self.key = (kind, layer) + at + ((sample.c,) if kind in ("max", "shift") else ())


def pre(b):
    return ([Step("scan", 0, b)] + [Step("tok", 0, b, n) for n in range(3)] + [Step("stash", 0, b)]
            + to_qkv(0, b))


def turned_steps(kind, layer, b, *n):
    return [Step(kind, layer, b, *n, c, half) for half in range(2) for c in range(KC)]


def norm(layer, b, n):
    return ([Step("stats", layer, b, n, half) for half in range(2)] + [Step("root", layer, b, n)]
            + [Step("apply", layer, b, n, half) for half in range(2)])


def cut(layer, b):
    def piece(kind, *at):
        return [Step(kind, layer, b, *at)]

    steps = []
    for w in range(2):
        steps += piece("qk", w, 0, 0) + piece("qk", w, 0, 1) + piece("qk", w, 1, 0) + piece("low", w, 0)
        if w == 1:
            steps += piece("pack", 0)
        steps += piece("qk", w, 1, 1) + piece("low", w, 1)
        if w == 0:
            steps += [Step("v", layer, b, n) for n in range(3)]
    return steps


def to_qkv(layer, b):
    n = 3 * layer
    steps = norm(layer, b, n) + turned_steps("xt", layer, b, n)
    if layer == 1:
        if b.k or b.c > 0:
            steps += fetch(1, b + -1)
        steps += [Step("qktok", 1, b, t) for t in range(NT)]
    return steps + cut(layer, b)


def project(layer, b):
    return turned_steps("ao", layer, b) + [Step("wo", layer, b, n) for n in range(3)]


def fetch(layer, b):
    return [Step("fetch", layer, b)]


def mid(b):
    return (project(0, b) + norm(0, b, 1) + turned_steps("xt", 0, b, 1) + norm(0, b, 2)
            + [Step("logit", 0, b), Step("gate", 0, b)] + turned_steps("xt", 0, b, 2)
            + [Step("mask", 0, b), Step("experts", 0, b)] + [Step("w2", 0, b, t) for t in range(NT)]
            + [Step("stash", 1, b)] + to_qkv(1, b))


def post(b):
    return (project(1, b) + norm(1, b, 4) + [Step("quant", 1, b, n) for n in range(3)] + [Step("qt", 1, b, c) for c in range(KC)]
            + [Step("ffn", 1, b, n) for n in range(3)] + [Step("store", 1, b)])


def pack(layer, b):
    return [Step("pack", layer, b, g) for g in range(1, NG)]


def first_pass(layer, b):
    steps, per = [], len(MAX_UNITS)
    for g in range(NG):
        steps += [Step("max", layer, b, g, u) for u in range(per)]
    for g in range(NG):
        steps.insert(min((g + 1) * per + 4, NG * per) + g, Step("shift", layer, b, g))
    head = per + 1 + LEAD
    return steps[:head], steps[head:]


def attention(layer, b, following=None):
    ahead = first_pass(layer, b)[1] + (first_pass(*following)[0] if following else [])
    rate = NG * (len(MAX_UNITS) + 1) / (NG * NCH * (GH + 1))
    steps, used, late, due = [], 0, None, 0.0
    kept = 5 if following else 0

    def add(step):
        nonlocal used, due
        steps.append(step)
        due += rate
        while used < min(len(ahead) - kept, int(due)):
            steps.append(ahead[used])
            used += 1

    for g in range(NG):
        for c in range(NCH):
            for j in range(GH):
                add(Step("scores", layer, b, g, c, j))
                if j == 2 and late:
                    add(late)
            late = Step("values", layer, b, g, c)
            if c == 2 and g > 0:
                steps += [Step("turn", layer, b, g - 1, half) for half in range(2)]
    return steps + [late] + ahead[used:] + [Step("turn", layer, b, NG - 1, half) for half in range(2)]


COST = {"max": 0.45, "scores": 0.25, "values": 0.95, "turn": 0.3, "shift": 0.2}


ROOM = {"stats": 0.6, "root": 2.0, "apply": 0.6, "mask": 2.0, "qt": 1.5, "low": 0.4, "load": 0.1, "stash": 0.0, "v": 0.9,
        "wo": 0.9, "qk": 0.9, "quant": 1.2, "ao": 0.5, "xt": 0.5}
FIRST = {("xt", 0, 0, 0): 2.0, ("xt", 1, 0, 0): 2.0, ("xt", 2, 0, 0): 2.0, ("xt", 3, 0, 0): 2.0, ("xt", 4, 0, 0): 2.0,
         ("wo", 0): 2.0, ("tok", 0): 3.0}


def places_of(stage, start, end):
    room = [ROOM.get(s.kind, 1.0) * FIRST.get((s.kind,) + s.at, 1.0) for s in stage]
    return [start + (end - start) * sum(room[1:i + 1]) / sum(room) for i in range(len(stage))]


def beside(att, stage, packs=(), then=()):
    until = STAGE_ENDS if then or packs else 0.85
    total = sum(COST[a.kind] for a in att)
    steps, done, later, packed, through, at = [], 0, 0, 0, 0, 0.0
    places, thens = places_of(stage, 0, until * total), places_of(then, until * total, 0.97 * total)
    for a in att:
        while done < len(stage) and places[done] <= at:
            steps.append(stage[done])
            done += 1
        while done == len(stage) and later < len(then) and thens[later] <= at:
            steps.append(then[later])
            later += 1
        steps.append(a)
        at += COST[a.kind]
        if a.kind == "scores" and a.at[1:] == (NCH - 1, GH - 1):
            through += 1
        while done == len(stage) and packed < min(through - 1, len(packs)):
            steps.append(packs[packed])
            packed += 1
    return steps + list(stage[done:]) + list(packs[packed:]) + list(then[later:])


def beside_own(att, stage, packs):
    return beside(att, [s for s in stage if s.kind != "v"], packs) + [s for s in stage if s.kind == "v"]


def number(layer, b):
    if layer == 0:
        return Affine(0, 0) if b.k == 0 and b.c == 0 else b.times(2) + -1
    return Affine(0, 2 * B - 1) if b.k == 0 and b.c == B - 1 else b.times(2) + 2


def with_experts(s, later):
    steps = []
    for m in range(4):
        for half in range(2):
            steps.append(Step("w1", s.layer, s.sample, m, half))
            for _ in range(BESIDE_W1):
                unit = next(t for t in later if t.kind in ("max", "shift"))
                later.remove(unit)
                steps.append(unit)
    return steps


class Section:

    def __init__(self, steps):
        self.steps = []
        waiting = list(steps)
        while waiting:
            s = waiting.pop(0)
            self.steps += with_experts(s, waiting) if s.kind == "experts" else [s]
        self.uses = {}
        for s in self.steps:
            if s.kind in SLOTTED:
                assert s.key not in self.uses
                self.uses[s.key] = len(self.uses)
        self.count = [(len(self.uses) + SLOTS - 1 - j) // SLOTS for j in range(SLOTS)]


def plan():
    def at(n):
        return Affine(0, n)

    def of_layer_0(i):
        return beside(attention(0, i, (1, i + -1)), mid(i + -1), pack(1, i + -1), (post(i + -2) if i.k or i.c > 1 else [])
                      + ([Step("load", 0, i + 1)] if i.k or i.c + 1 < B else []))

    def of_layer_1(i):
        return beside(attention(1, i + -1, (0, i + 1)), pre(i + 1), pack(0, i + 1), fetch(0, i))

    start = [Section([Step("load", 0, at(0)), Step("scan", 0, at(0)), Step("setup", 0, at(0))] + pre(at(0))[1:] + [Step("load", 0, at(1))] + pack(0, at(0))),
             Section(first_pass(0, at(0))[0] + beside_own(attention(0, at(0), (0, at(1))), pre(at(1)), pack(0, at(1))) + fetch(0, at(0))),
             Section(of_layer_0(at(1))), Section(of_layer_1(at(1)))]
    loop = [Section(of_layer_0(Affine(1, 0))), Section(of_layer_1(Affine(1, 0)))]
    end = [Section(of_layer_0(at(B - 1))),
           Section(fetch(0, at(B - 1)) + beside_own(attention(1, at(B - 2), (1, at(B - 1))), mid(at(B - 1)), pack(1, at(B - 1)))),
           Section(beside(attention(1, at(B - 1)), post(at(B - 2)))),
           Section(fetch(1, at(B - 1)) + post(at(B - 1)))]
    lo, hi = 2, B - 1
    before = [0] * SLOTS
    for s in start:
        s.before = [Affine(0, n) for n in before]
        before = [n + c for n, c in zip(before, s.count)]
    per = [sum(s.count[j] for s in loop) for j in range(SLOTS)]
    at_turn = [Affine(per[j], before[j] - lo * per[j]) for j in range(SLOTS)]
    for s in loop:
        s.before = list(at_turn)
        at_turn = [a + c for a, c in zip(at_turn, s.count)]
    before = [n + (hi - lo) * p for n, p in zip(before, per)]
    for s in end:
        s.before = [Affine(0, n) for n in before]
        before = [n + c for n, c in zip(before, s.count)]
    return start, loop, end, lo, hi


START, LOOP, END, LO, HI = plan()


def tower(nc, x, W, b, Wqvk, Wo0, Wg, ln_scale, ln_bias, W1, b1, W2, b2, Wqkv, Wo1, rhs,
          ident, causal, cosines, sines, pick, out):
    ctx = ExitStack()
    with ctx:
        def sb(name, shape, dt=F32):
            return ctx.enter_context(nc.sbuf_tensor(name, shape, dt))

        def sem(name):
            return ctx.enter_context(nc.semaphore(name))

        stash = nc.dram_tensor("stash", (2, B, TB, NT, D), F32, kind="Internal").ap()
        spread = nc.dram_tensor("spread", (2, 2, 3, D, T), BF16, kind="Internal").ap()

        probs_raw = sb("probs", [128, RING * GH * CUT])
        probs = probs_raw[0:TB, :].rearrange("p (r n) -> p r n", n=CUT)
        early = [0]

        def early_weight(rows, *dims):
            n = int(np.prod(dims))
            v = probs_raw[0:rows, early[0]:early[0] + n]
            early[0] += n
            assert early[0] <= RING * GH * CUT
            letters = "abcd"[:len(dims)]
            sizes = {c: d for c, d in zip(letters, dims)}
            return v.rearrange(f"p ({' '.join(letters)}) -> p {' '.join(letters)}", **sizes) if len(dims) > 1 else v

        pickf = early_weight(32, 4, 128)
        maskf = early_weight(TB, TB)
        w_tok = early_weight(128, KC, 128)
        w_g = early_weight(E, D)
        lns = early_weight(E, 2, D)
        w_1 = early_weight(128, KC, E, HID)
        b_2 = early_weight(E, D)
        b_2r = early_weight(E, D)
        w_raw = early_weight(128, 6, D)
        rhs_t = early_weight(128, KC, D)

        identf = sb("identf", [128, 128])
        identb = sb("identb", [128, 128], BF16)
        maskb = sb("maskb", [TB, TB], BF16)
        cos_sb = sb("cos_sb", [TB, NT, DH])
        sin_sb = sb("sin_sb", [TB, NT, DH])
        pickb = sb("pickb", [32, 4, 128], BF16)
        decay = sb("decay", [128, 1])
        ones = sb("ones", [128, TB])
        neghalf = sb("neghalf", [TB, NT])
        rank = sb("rank", [TB, E])
        wt_tok = sb("wt_tok", [128, D])
        b_tok = sb("b_tok", [TB, D])
        w_qvk = sb("w_qvk", [128, KC, 3 * D])
        w_o0 = sb("w_o0", [128, KC, D])
        wt_g = sb("wt_g", [128, KC, E])
        lnt = sb("lnt", [128, 2, KC, E])
        w_1s = sb("w_1s", [128, KC, E * HID])
        b_1 = sb("b_1", [128, 4])
        b_1e = sb("b_1e", [128, 4])
        w_2 = sb("w_2", [128, 4, D])
        b_2s = sb("b_2s", [32, D], BF16)
        w_qkv = sb("w_qkv", [128, KC, 3 * D])
        w_o1t = sb("w_o1t", [128, KC, D])
        r_abs = sb("r_abs", [128, 3, KC])
        rq = sb("rq", [128, KC, D], BF16)
        r_scale = sb("r_scale", [TB, D])

        res = sb("res", [TB, NT, D])
        stats = sb("stats", [TB, NT, 6])
        mv = sb("mv", [TB, NT, 2])
        veps = sb("veps", [TB, NT])
        rstd = sb("rstd", [TB, NT])
        xn = sb("xn", [TB, NT, D])
        xh = sb("xh", [TB, NT, D])
        ao = [sb(f"ao{n}", [TB, NT, D]) for n in range(2)]
        xt = sb("xt", [128, KC, T])
        rest = sb("rest", [128, 2, T])
        xs, bwd = rest[:, 0, :], rest[:, 1, :]
        parts = sb("parts", [128, 2, 3, T], BF16)
        rq_t = parts[:, 0, 0, 0:2 * D].rearrange("p (c n) -> p c n", c=KC)
        b_2p = parts[0:E, 1, :, 0:D]
        qp = sb("qp", [SROWS, H, T], BF16)
        kp = sb("kp", [SROWS, H, T], BF16)
        va = [sb(f"va{n}", [TB, NT, H, DH + 1]) for n in range(2)]
        mx = sb("mx", [TB, 2, GH, NT])
        mx2 = sb("mx2", [TB, GH, NT - SPLIT, 2])
        ms = sb("ms", [TB, 2, 3, GH * NT], BF16)
        mr = sb("mr", [TB, GH * NT])
        mt = sb("mt", [3 * GH * NT, 2, TB], BF16)
        os_ = sb("os", [128, T])
        rden = sb("rden", [TB, NT, GH])
        hidden = sb("hidden", [128, NT * 2 * D])
        ghid = hidden[:, 0:4 * T].rearrange("p (m t) -> p m t", m=4)
        qr = hidden[0:TB, :].rearrange("p (t n) -> p t n", t=NT)
        xin, fwd = hidden[:, 0:T], hidden[:, T:2 * T]
        w_o1 = hidden[:, 2 * T:2 * T + KC * D].rearrange("p (c n) -> p c n", c=KC)
        r_diag = hidden[:, 2 * T + KC * D:2 * T + KC * (D + 128)].rearrange("p (c n) -> p c n", c=KC)
        qb = hidden[0:TB, 2 * T:2 * T + NT * D // 2].bitcast(BF16).rearrange("p (t n) -> p t n", t=NT)
        scratch = sb("scratch", [128, 4 * D])
        rot = scratch[0:TB, :].rearrange("p (a n) -> p a n", a=2)
        qbt = scratch[:, 0:KC * T // 2].bitcast(BF16).rearrange("p (c t) -> p c t", c=KC)
        lg = sb("lg", [TB, NT, E])
        lgm = sb("lgm", [TB, 2, NT])
        sel = sb("sel", [TB, NT, E])
        mk = sb("mk", [TB, NT, 32], BF16)
        mkt = sb("mkt", [32, NT, TB], BF16)
        am = sb("am", [TB, 3, NT])

        slot = [ctx.enter_context(nc.psum_tensor(f"slot{i}", [128, 2, 512], F32)) for i in range(2)]
        st = [ctx.enter_context(nc.psum_tensor(f"st{i}", [128, 512], F32)) for i in range(2)]
        acc = ctx.enter_context(nc.psum_tensor("acc", [128, 2, 512], F32))
        bank = [slot[i // 2][:, i % 2:i % 2 + 1, :] for i in range(SLOTS)]
        bankb = [slot[i // 2][:].bitcast(BF16)[:, i % 2:i % 2 + 1, :] for i in range(SLOTS)]
        stb = [s[:].bitcast(BF16) for s in st]

        signals = []

        class Signal:

            def __init__(self, name, per):
                self.sem, self.per = sem(name), per
                signals.append(self)

        turn = {}
        stands_apart = []
        s_waited = sem("waited")

        def stand_apart(eng):
            eng.sem_inc(s_waited, 1)

        def wait_at(eng, signal, at):
            value = at.c + 1
            if at.k:
                eng.wait_ge(signal.sem, turn[eng] * at.k + value)
                if eng in stands_apart:
                    stand_apart(eng)
            else:
                eng.wait_ge(signal.sem, value)

        def need(eng, signal, sample, n):
            wait_at(eng, signal, sample.times(signal.per) + n)

        def cut_before(layer, b, other):
            if layer == other:
                return b
            if layer == 1:
                return b + 2 if b.k or b.c + 1 < B else b + 1
            return b + -1 if b.k or b.c > 0 else b

        full = [Signal(f"slot{i}_full", None) for i in range(SLOTS)]
        done = [Signal(f"slot{i}_done", None) for i in range(SLOTS)]
        s_weights = sem("weights_loaded")
        s_setup = {n: sem(f"setup_{n}") for n in ("pool", "act", "dve", "pe", "b2", "side")}
        s_x = Signal("x_loaded", 16)
        s_xs = Signal("x_scaled", 1)
        s_scan = Signal("scanned", 3)
        s_ewma = Signal("ewma_ready", 1)
        s_stashed = [Signal(f"stashed{n}", 16) for n in range(2)]
        s_fetched = [Signal(f"fetched{n}", 16) for n in range(2)]
        s_stats = [Signal(f"norm{n}_stats", 1) for n in range(5)]
        s_mv = [Signal(f"norm{n}_moments", 1) for n in range(5)]
        s_veps = [Signal(f"norm{n}_veps", 1) for n in range(5)]
        s_rstd = [Signal(f"norm{n}_rstd", 1) for n in range(5)]
        s_norm = [Signal(f"norm{n}_done", NT) for n in range(5)]
        s_high = [Signal(f"part_high{n}", 4 * KC) for n in range(2)]
        s_mid = [Signal(f"part_mid{n}", 4 * KC) for n in range(2)]
        s_low = [Signal(f"part_low{n}", 2 * KC) for n in range(2)]
        s_spread = [[Signal(f"spread{n}_{c}", 2 * 16) for c in range(KC)] for n in range(2)]
        s_packed = [Signal(f"packed{g}", 2 * NSTRIP * 16) for g in range(NG)]
        s_ms = Signal("shift_parts", NG * 5)
        s_mrow = [Signal(f"shift_row{i}", (NG // 2) * 16) for i in range(2)]
        s_scores = Signal("scores_ready", NG * NCH * GH)
        s_exp = Signal("exp_done", NG * NCH * GH)
        s_masked = Signal("masked", NG * NMASKED)
        s_pv = Signal("values_summed", NG * NCH)
        s_osb = Signal("sums_copied", NG)
        s_rden = Signal("denominators", NG * 2)
        s_qr = Signal("rotary_done", NT)
        s_gate = Signal("gate_steps", 5)
        s_mk = Signal("gate_masks", 2)
        s_amax = Signal("quant_scale", 3)
        s_quant = Signal("quant_steps", NT + 2)
        s_out = Signal("result_ready", 1)
        s_stored = Signal("stored", 16)

        here = {}

        def await_done(eng, *keys, free=None, before=False):
            s = here[eng]
            at = {i: 0 for i in range(SLOTS)} if before else {}
            for k in [s.uses[key] for key in keys] + ([] if free is None else [s.uses[free] - SLOTS]):
                at[k % SLOTS] = max(at.get(k % SLOTS, 0), k // SLOTS + 1)
            for i, n in at.items():
                wait_at(eng, done[i], s.before[i] + n)

        def take(eng, step, *results, before=False):
            await_done(eng, *results, free=step.key, before=before)
            return bank[here[eng].uses[step.key] % SLOTS]

        def filled(eng, ins, step):
            ins.then_inc(full[here[eng].uses[step.key] % SLOTS].sem, 1)

        def await_full(eng, key):
            s = here[eng]
            k = s.uses[key]
            wait_at(eng, full[k % SLOTS], s.before[k % SLOTS] + (k // SLOTS + 1))
            return bank[k % SLOTS]

        def consumed(eng, ins, step):
            ins.then_inc(done[here[eng].uses[step.key] % SLOTS].sem, 1)

        def low_view(eng, step):
            return bankb[here[eng].uses[step.key] % SLOTS]

        def walk(eng, doing):
            def sections(those):
                for here[eng] in those:
                    for s in here[eng].steps:
                        if s.kind in doing:
                            doing[s.kind](s, s.layer, s.sample, *s.at)

            sections(START)
            with eng.Fori(LO, HI) as i:
                turn[eng] = i
                sections(LOOP)
            sections(END)

        weights = [
            (identf[:], ident), (maskf, causal),
            (cos_sb[:], cosines.rearrange("(t p) d -> p t d", p=TB)),
            (sin_sb[:], sines.rearrange("(t p) d -> p t d", p=TB)),
            (pickf, pick),
            (w_tok, W.rearrange("(c p) i -> p c i", p=128)),
            (b_tok[:], b.partition_broadcast(TB)),
            (w_qvk[:], Wqvk.rearrange("(c p) n -> p c n", p=128)),
            (w_o0[:], Wo0.rearrange("(c p) n -> p c n", p=128)),
            (w_g, Wg), (lns[:, 0, :], ln_scale), (lns[:, 1, :], ln_bias),
            (b_2, b2),
            (w_2[:], W2.rearrange("(c e) h n -> (e h) c n", e=2)),
            (w_raw, Wqkv.rearrange("(c p) n -> p c n", p=128)),
            (w_o1, Wo1.rearrange("(c p) n -> p c n", p=128)),
            (rhs_t, rhs.rearrange("(c p) n -> p c n", p=128)),
        ]
        for c in range(KC):
            weights.append((w_1[:, c], W1.rearrange("e (c p) h -> c p e h", p=128)[c]))
        for c in range(4):
            weights.append((b_1[:, c:c + 1], b1.rearrange("(c e) h -> c (e h)", e=2)[c].rearrange("(p a) -> p a", a=1)))
        n_weights = 16 * len(weights)

        block = ctx.enter_context(nc.Block())

        @block.sync
        def _(sp):
            def of_sample(dram, b):
                if b.k:
                    return dram[bass.ds(turn[sp] + b.c, 1)].rearrange("a p t d -> p (a t) d")
                return dram[b.c]

            def setup(s, layer, b):
                for dst, src in weights:
                    sp.dma_start(dst, src).then_inc(s_weights, 16)
                sp.wait_ge(s_setup["dve"], 11)
                sp.wait_ge(s_setup["pool"], 5)
                for p in range(3):
                    sp.dma_start(b_2s[p * E:(p + 1) * E, :], b_2p[:, p, :]).then_inc(s_setup["b2"], 16)
                sp.wait_ge(s_setup["b2"], 48)
                sp.wait_ge(s_setup["pe"], 9)

            def load(s, layer, b):
                await_done(sp, *[k for k in here[sp].uses if k[:2] == ("qk", 1)])
                need(sp, s_ewma, b, 0)
                xv = x[bass.ds(turn[sp] + b.c, 1)].rearrange("a c t -> (a c) t") if b.k else x[b.c]
                sp.dma_start(xin, xv).then_inc(s_x.sem, 16)

            def stash_(s, layer, b):
                key = ("tok", 0, 2) if layer == 0 else ("w2", 0, NT - 1)
                await_done(sp, key)
                sp.dma_start(of_sample(stash[layer], b), res[:]).then_inc(s_stashed[layer].sem, 16)

            def fetch(s, layer, b):
                need(sp, s_stashed[layer], b, 16)
                if b.k or b.c + 1 < B:
                    need(sp, s_stashed[layer], b + 1, 16)
                    need(sp, s_norm[3 * layer], b + 1, NT)
                else:
                    need(sp, s_stored, b + (layer - 2), 16)
                sp.dma_start(res[:], of_sample(stash[layer], b)).then_inc(s_fetched[layer].sem, 16)

            def low(s, layer, b, w, c):
                need(sp, s_low[layer], b, w * KC + c + 1)
                if w == 0 and c == 0 and (b.k or b.c > 0):
                    for g in range(NG):
                        need(sp, s_packed[g], number(layer, b + -1), 2 * NSTRIP * 16)
                sp.dma_start(spread[layer, w].rearrange("q (c p) t -> c p q t", c=KC)[c],
                             parts[:, c, :, :]).then_inc(s_spread[layer][c].sem, 16)

            def pack(s, layer, b, g):
                if g % 2 == 0:
                    need(sp, s_spread[layer][g // 2], b, 32)
                a = number(layer, b)
                if a.k or a.c > 0:
                    need(sp, s_scores, a + -1, (g + 1) * NCH * GH)
                for w in range(2):
                    for strip, part in enumerate((Q_PARTS, K_PARTS)[w]):
                        sp.dma_start((qp, kp)[w][strip * DH:(strip + 1) * DH, g * GH:(g + 1) * GH, :],
                                     spread[layer, w, part].rearrange("(h d) t -> d h t", d=DH)[:, g * GH:(g + 1) * GH, :])\
                            .then_inc(s_packed[g].sem, 16)

            def shift(s, layer, b, g):
                await_done(sp, s.key)
                sp.dma_start(qp[KROWS:SROWS, g * GH:(g + 1) * GH, :], mt[:, g % 2, :])\
                    .then_inc(s_mrow[g % 2].sem, 16)

            def store(s, layer, b):
                need(sp, s_out, b, 1)
                sp.dma_start(of_sample(out.rearrange("b (t p) d -> b p t d", p=TB), b), res[:]).then_inc(s_stored.sem, 16)

            for signal in signals:
                sp.sem_inc(signal.sem, 1)
            stands_apart.append(sp)
            walk(sp, {"setup": setup, "load": load, "stash": stash_, "fetch": fetch, "low": low, "pack": pack, "shift": shift,
                      "store": store})
            sp.wait_ge(s_stored.sem, B * 16 + 1)

        @block.tensor
        def _(pe):
            mm = nc.tensor.matmul

            def setup(s, layer, b):
                pe.wait_ge(s_weights, n_weights)
                pe.wait_ge(s_setup["pool"], 7)
                a = slot[0]
                for c in range(KC):
                    last = nc.tensor.transpose(a[:, 0, c * 128:(c + 1) * 128], w_tok[:, c, :], identf[:])
                last.then_inc(s_setup["pe"], 1)
                for c in range(KC):
                    cols = slice(c * 128, (c + 1) * 128)
                    nc.tensor.transpose(a[:, 1, c * 8:c * 8 + 8], w_g[:, cols], identf[0:E, 0:E])
                    for v in range(2):
                        o = 16 + v * 16 + c * 8
                        last = nc.tensor.transpose(a[:, 1, o:o + 8], lns[:, v, cols], identf[0:E, 0:E])
                last.then_inc(s_setup["pe"], 1)
                for c in range(KC):
                    s = slot[1]
                    if c:
                        pe.wait_ge(s_setup["act"], 3)
                    for r in range(6):
                        last = nc.tensor.transpose(s[:, r // 3, r % 3 * 128:r % 3 * 128 + 128],
                                                   w_raw[:, r, c * 128:(c + 1) * 128], identf[:])
                    last.then_inc(s_setup["pe"], 1)
                for c in range(KC):
                    for r in range(KC):
                        last = nc.tensor.transpose(st[0][:, (c * KC + r) * 128:(c * KC + r + 1) * 128],
                                                   w_o1[:, r, c * 128:(c + 1) * 128], identf[:])
                last.then_inc(s_setup["pe"], 1)
                for c in range(KC):
                    for r in range(KC):
                        last = nc.tensor.transpose(st[1][:, (c * KC + r) * 128:(c * KC + r + 1) * 128],
                                                   rhs_t[:, r, c * 128:(c + 1) * 128], identf[:])
                last.then_inc(s_setup["pe"], 1)
                pe.wait_ge(s_setup["act"], 2)
                pe.wait_ge(s_setup["dve"], 1)
                for e in range(E):
                    for c in range(KC):
                        last = mm(acc[64 * (e % 2):64 * (e % 2) + 64, 0, e // 2:e // 2 + 1],
                                  w_1[:, c, e, :], lnt[:, 1, c, e:e + 1], start=(c == 0), stop=(c == KC - 1))
                last.then_inc(s_setup["pe"], 1)
                pe.wait_ge(s_setup["dve"], 8)
                pe.wait_ge(s_setup["act"], 5)
                for c in range(KC):
                    for r in range(KC):
                        last = nc.tensor.transpose(stb[0][:, (c * KC + r) * 128:(c * KC + r + 1) * 128],
                                                   rq_t[:, r, c * 128:(c + 1) * 128], identb[:])
                last.then_inc(s_setup["pe"], 1)
                for c in range(KC):
                    last = mm(acc[0:TB, 1, c * 128:(c + 1) * 128], ones[:], r_diag[:, c, :], start=True, stop=True)
                last.then_inc(s_setup["pe"], 1)
                pe.wait_ge(s_setup["dve"], 12)
                pe.wait_ge(s_setup["act"], 8)
                pe.wait_ge(s_setup["b2"], 48)

            def turned(s, src, c, half, ready, results=(), before=False):
                o = take(pe, s, *results, before=before)
                for j in range(3):
                    ready(3 * half + j)
                    last = nc.tensor.transpose(o[:, 0, j * TB:(j + 1) * TB],
                                               src[:, 3 * half + j, c * 128:(c + 1) * 128], identf[0:TB, 0:TB])
                filled(pe, last, s)

            def by_blocks(s, after, n, lhs, rhs_of, nk, more=None, per=2):
                o = take(pe, s, *after)
                for j in range(per):
                    t = n * per + j
                    to = o[0:TB, 0, j * D:(j + 1) * D]
                    for c in range(nk):
                        last = mm(to, lhs[:, c, t * TB:(t + 1) * TB], rhs_of(c), start=(c == 0),
                                  stop=(c == nk - 1 and more is None))
                    if more is not None:
                        last = mm(to, more[0][:, t, :], more[1], start=False, stop=True)
                filled(pe, last, s)

            def features_by(s, after, half, weight, extra=None):
                o = take(pe, s, *after)
                for c in range(KC):
                    last = mm(o[:, 0, 0:HALF], weight(c), xt[:, c, half * HALF:(half + 1) * HALF],
                              start=(c == 0), stop=(c == KC - 1 and extra is None))
                if extra is not None:
                    last = mm(o[:, 0, 0:HALF], extra,
                              mkt[:, half * 3:half * 3 + 3, :].rearrange("p a b -> p (a b)"), start=False, stop=True)
                filled(pe, last, s)

            def both(kind, layer, *at):
                return [(kind, layer) + at + (c, half) for c in range(KC) for half in range(2)]

            def max_(s, layer, b, g, u):
                if u == 0:
                    need(pe, s_packed[g], number(layer, b), 2 * NSTRIP * 16)
                i, h0, nh, k0, n = MAX_UNITS[u]
                o = take(pe, s)
                diag = k0 + n == (i + 1) * TB
                for j in range(nh):
                    h = g * GH + h0 + j
                    last = mm(o[0:TB, 0, j * n:(j + 1) * n], qp[0:KROWS, h, i * TB:(i + 1) * TB],
                              kp[0:KROWS, h, k0:k0 + n], start=True, stop=not diag, skip_group_check=True)
                    if diag:
                        last = mm(o[0:TB, 0, (j + 1) * n - TB:(j + 1) * n], identb[0:TB, 0:TB], maskb[:],
                                  start=False, stop=True, skip_group_check=True)
                filled(pe, last, s)

            def shift(s, layer, b, g):
                take(pe, s)
                need(pe, s_ms, number(layer, b), (g + 1) * 5)
                filled(pe, nc.tensor.transpose(low_view(pe, s)[0:3 * GH * NT, 0, 0:TB],
                                               ms[:, g % 2, :, :].rearrange("p a b -> p (a b)"),
                                               identb[0:TB, 0:TB]), s)

            def scores(s, layer, b, g, c, j):
                a = number(layer, b)
                if c == 0 and j == 0:
                    need(pe, s_mrow[g % 2], a, (g // 2 + 1) * 16)
                n = (g * NCH + c) * GH + j
                h = g * GH + j
                need(pe, s_exp, a, max(n - 1, 0))
                for kb, q0, q1, col in CHUNKS[c]:
                    last = mm(st[n % 2][0:TB, col:col + q1 - q0], kp[:, h, kb * TB:(kb + 1) * TB],
                              qp[:, h, q0:q1], start=True, stop=True, skip_group_check=True)
                last.then_inc(s_scores.sem, 1)

            def values(s, layer, b, g, c):
                a = number(layer, b)
                n = g * NCH + c
                if DIAGONAL[c] is None:
                    need(pe, s_exp, a, (n + 1) * GH)
                else:
                    need(pe, s_masked, a, g * NMASKED + sum(d is not None for d in DIAGONAL[:c + 1]) * GH)
                if c == 0:
                    need(pe, s_osb, a, g)
                for kb, q0, q1, col in CHUNKS[c]:
                    for f, z in ((q0, min(q1, CUT)), (max(q0, CUT), q1)):
                        if f >= z:
                            continue
                        bank = int(f >= CUT)
                        for j in range(GH):
                            ring = n % RING * GH + j
                            last = mm(acc[32 * j:32 * j + DH + 1, bank, f - CUT * bank:z - CUT * bank],
                                      va[layer][:, kb, g * GH + j, :],
                                      probs[:, ring, col + f - q0:col + z - q0],
                                      start=(kb == 0), stop=False, skip_group_check=True)
                last.then_inc(s_pv.sem, 1)

            def turn_(s, layer, b, g, half):
                o = take(pe, s)
                need(pe, s_osb, number(layer, b), g + 1)
                for j in range(3):
                    t = 3 * half + j
                    last = nc.tensor.transpose(o[0:TB, 0, j * 128:(j + 1) * 128], os_[:, t * TB:(t + 1) * TB], identf[:])
                filled(pe, last, s)

            def tok(s, layer, b, n):
                o = take(pe, s)
                need(pe, s_ewma, b, 1)
                for j in range(2):
                    t = n * 2 + j
                    last = mm(o[0:TB, 0, j * D:(j + 1) * D], fwd[:, t * TB:(t + 1) * TB], wt_tok[:], start=True, stop=True)
                filled(pe, last, s)

            def xt_(s, layer, b, n, c, half):
                turned(s, xh if n == 2 else xn, c, half, lambda t: need(pe, s_norm[n], b, t + 1) if c == 0 else None)

            def qk(s, layer, b, w, c, half):
                if layer == 0:
                    col = w * 2 * D + c * 128
                    features_by(s, both("xt", 0, 0), half, lambda k: w_qvk[:, k, col:col + 128])
                    return
                o = take(pe, s)
                if w == 0 and c == 0:
                    need(pe, s_qr, b, 3 * half + 3)
                for j in range(3):
                    col = w * D + c * 128
                    last = nc.tensor.transpose(o[:, 0, j * TB:(j + 1) * TB], qr[:, 3 * half + j, col:col + 128],
                                               identf[0:TB, 0:TB])
                filled(pe, last, s)

            def v(s, layer, b, n):
                w, col = ((w_qvk, D), (w_qkv, 2 * D))[layer]
                by_blocks(s, both("xt", layer, 3 * layer), n, xt, lambda c: w[:, c, col:col + D], KC)

            def ao_(s, layer, b, c, half):
                turned(s, ao[layer], c, half, lambda t: None, before=True)

            def wo(s, layer, b, n):
                w = (w_o0, w_o1t)[layer]
                by_blocks(s, both("ao", layer), n, xt, lambda c: w[:, c, :], KC)

            def logit(s, layer, b):
                o = take(pe, s, *both("xt", 0, 1))
                for t in range(NT):
                    for c in range(KC):
                        last = mm(o[0:TB, 0, t * E:(t + 1) * E], xt[:, c, t * TB:(t + 1) * TB], wt_g[:, c, :],
                                  start=(c == 0), stop=(c == KC - 1))
                filled(pe, last, s)

            def mask(s, layer, b):
                take(pe, s)
                need(pe, s_mk, b, 2)
                for t in range(NT):
                    last = nc.tensor.transpose(low_view(pe, s)[0:32, 0, t * 128:t * 128 + TB],
                                               mk[:, t, :], identb[0:TB, 0:TB])
                filled(pe, last, s)

            def w1(s, layer, b, m, half):
                features_by(s, [("mask", 0)] + both("xt", 0, 2), half, lambda k: w_1s[:, k, m * 128:(m + 1) * 128],
                            pickb[:, m, :])

            def w2(s, layer, b, n):
                by_blocks(s, [("w1", 0, m, half) for m in range(4) for half in range(2)], n, ghid, lambda c: w_2[:, c, :],
                          4, (mkt, b_2s[:]), per=1)

            def qktok(s, layer, b, t):
                o = take(pe, s, *both("xt", 1, 3))
                for c in range(KC):
                    last = mm(o[0:TB, 0, :], xt[:, c, t * TB:(t + 1) * TB], w_qkv[:, c, 0:2 * D],
                              start=(c == 0), stop=(c == KC - 1))
                filled(pe, last, s)

            def qt(s, layer, b, c):
                take(pe, s)
                need(pe, s_quant, b, NT + 2)
                for t in range(NT):
                    last = nc.tensor.transpose(low_view(pe, s)[:, 0, t * 128:t * 128 + TB],
                                               qb[:, t, c * 128:(c + 1) * 128], identb[0:TB, 0:TB])
                filled(pe, last, s)

            def ffn(s, layer, b, n):
                by_blocks(s, [("qt", 1, c) for c in range(KC)], n, qbt, lambda c: rq[:, c, :], KC)

            walk(pe, {"setup": setup, "max": max_, "shift": shift, "scores": scores, "values": values, "turn": turn_, "tok": tok, "xt": xt_,
                      "qk": qk, "v": v, "ao": ao_, "wo": wo, "logit": logit, "mask": mask, "w1": w1, "w2": w2,
                      "qktok": qktok, "qt": qt, "ffn": ffn})

        @block.scalar
        def _(act):
            def copy(o, i):
                return nc.scalar.activation(o, i, ACT.Copy)

            def setup(s, layer, b):
                act.wait_ge(s_setup["pe"], 1)
                nc.scalar.mul(wt_tok[:], slot[0][:, 0, 0:D], 0.5).then_inc(s_setup["act"], 1)
                act.wait_ge(s_setup["pe"], 2)
                copy(wt_g[:].rearrange("p c e -> p (c e)"), slot[0][:, 1, 0:16])
                copy(lnt[:].rearrange("p a c e -> p (a c e)"), slot[0][:, 1, 16:48]).then_inc(s_setup["act"], 1)
                for c in range(KC):
                    act.wait_ge(s_setup["pe"], 3 + c)
                    copy(w_qkv[:, c, :].rearrange("p (a n) -> p a n", a=2), slot[1][:, :, 0:384])\
                        .then_inc(s_setup["act"], 1)
                act.wait_ge(s_setup["pe"], 5)
                copy(w_o1t[:].rearrange("p c n -> p (c n)"), st[0][:]).then_inc(s_setup["act"], 1)
                act.wait_ge(s_setup["pe"], 7)
                copy(b_1e[:], acc[:, 0, 0:4]).then_inc(s_setup["act"], 1)
                act.wait_ge(s_setup["pe"], 8)
                copy(rq[:].rearrange("p c n -> p (c n)"), stb[0][:, 0:2 * D]).then_inc(s_setup["act"], 1)
                act.wait_ge(s_setup["pe"], 9)
                copy(r_scale[:], acc[0:TB, 1, 0:D]).then_inc(s_setup["act"], 1)

            def copy_turned(s, c, half):
                o = await_full(act, s.key)
                consumed(act, copy(xt[:, c, half * HALF:(half + 1) * HALF], o[:, 0, 0:HALF]), s)

            def v(s, layer, b, n):
                o = await_full(act, s.key)
                to = va[layer]
                consumed(act, copy(to[:, n * 2:n * 2 + 2, :, 0:DH],
                                   o[0:TB, 0, :].rearrange("p (t h d) -> p t h d", t=2, h=H)), s)

            def qk(s, layer, b, w, c, half):
                o = await_full(act, s.key)
                if half == 0 and w == 0:
                    for other in range(2):
                        need(act, s_spread[other][c], cut_before(layer, b, other), 0)
                if half == 0 and w == 1:
                    need(act, s_spread[layer][c], b, 16)
                copy(parts[:, c, 0, half * HALF:(half + 1) * HALF], o[:, 0, 0:HALF]).then_inc(s_high[layer].sem, 1)

            def shift(s, layer, b, g):
                await_full(act, s.key)
                need(act, s_mrow[g % 2], number(layer, b), g // 2 * 16)
                consumed(act, copy(mt[:, g % 2, :], low_view(act, s)[0:3 * GH * NT, 0, 0:TB]), s)

            def scores(s, layer, b, g, c, j):
                scale = (1.0 / 16.0, 0.25)[layer]
                a = number(layer, b)
                k = g * NCH + c
                n = k * GH + j
                if j == 0:
                    need(act, s_pv, a, max(k - RING + 1, 0))
                need(act, s_scores, a, n + 1)
                nc.scalar.activation(probs[:, k % RING * GH + j, 0:WIDTH[c]], st[n % 2][0:TB, 0:WIDTH[c]],
                                     ACT.Exp, scale=scale).then_inc(s_exp.sem, 1)

            def values(s, layer, b, g, c):
                if c < NCH - 1:
                    return
                need(act, s_pv, number(layer, b), (g + 1) * NCH)
                if g > 0:
                    await_full(act, ("turn", layer, g - 1, 1))
                copy(os_[:, 0:CUT], acc[:, 0, 0:CUT])
                copy(os_[:, CUT:T], acc[:, 1, 0:T - CUT]).then_inc(s_osb.sem, 1)

            def mask(s, layer, b):
                await_full(act, s.key)
                rows = low_view(act, s)[0:32, 0, 0:NT * 128].rearrange("p (t n) -> p t n", t=NT)
                consumed(act, copy(mkt[:], rows[:, :, 0:TB]), s)

            def w1(s, layer, b, m, half):
                o = await_full(act, s.key)
                consumed(act, nc.scalar.activation(ghid[:, m, half * HALF:(half + 1) * HALF], o[:, 0, 0:HALF],
                                                   ACT.Gelu, bias=b_1[:, m:m + 1]), s)

            def qt(s, layer, b, c):
                await_full(act, s.key)
                rows = low_view(act, s)[:, 0, 0:NT * 128].rearrange("p (t n) -> p t n", t=NT)
                consumed(act, copy(qbt[:, c, :].rearrange("p (t n) -> p t n", t=NT), rows[:, :, 0:TB]), s)

            walk(act, {"setup": setup, "xt": lambda s, layer, b, n, c, half: copy_turned(s, c, half),
                       "ao": lambda s, layer, b, c, half: copy_turned(s, c, half), "v": v, "qk": qk, "shift": shift,
                       "scores": scores, "values": values, "mask": mask, "w1": w1, "qt": qt})

        @block.gpsimd
        def _(pool):
            def setup(s, layer, b):
                g = nc.gpsimd
                g.memset(decay[:], 1.0 - ALPHA).then_inc(s_setup["pool"], 1)
                g.memset(ones[:], 1.0).then_inc(s_setup["pool"], 1)
                g.memset(neghalf[:], -0.5).then_inc(s_setup["pool"], 1)
                for layer in range(2):
                    last = g.memset(va[layer][:], 1.0)
                last.then_inc(s_setup["pool"], 1)
                g.memset(b_2s[:], 0.0).then_inc(s_setup["pool"], 1)
                for e in range(E):
                    last = g.memset(rank[:, e:e + 1], float(E - e))
                last.then_inc(s_setup["pool"], 1)
                g.memset(rden[:], 0.0).then_inc(s_setup["pool"], 1)

            def root(s, layer, b, n):
                need(pool, s_mv[n], b, 1)
                nc.gpsimd.tensor_scalar(veps[:], mv[:, :, 1], EPS, None, ALU.add).then_inc(s_veps[n].sem, 1)
                need(pool, s_veps[n], b, 1)
                nc.gpsimd.tensor_tensor(rstd[:], veps[:], neghalf[:], ALU.pow).then_inc(s_rstd[n].sem, 1)

            def scores(s, layer, b, g, c, j):
                if DIAGONAL[c] is None:
                    return
                k = g * NCH + c
                need(pool, s_exp, number(layer, b), k * GH + j + 1)
                p = probs[:, k % RING * GH + j, :]
                if c == 2:
                    o, pattern = p[:, 0:500].rearrange("p (a n) -> p a n", a=4)[:, 0::3, :], [[0, 2], [1, TB]]
                else:
                    o, pattern = p[:, 0:TB], [[1, TB]]
                nc.gpsimd.affine_select(out=o, in_=o, compare_op=ALU.is_ge, fill=0.0, base=0,
                                        pattern=pattern, channel_multiplier=-1).then_inc(s_masked.sem, 1)

            stands_apart.append(pool)
            walk(pool, {"setup": setup, "root": root, "scores": scores})

        @block.vector
        def _(dve):
            v = nc.vector

            def setup(s, layer, b):
                n, side = s_setup["dve"], s_setup["side"]
                v.memset(acc[:], 0.0).then_inc(n, 1)
                dve.wait_ge(s_weights, n_weights)
                v.tensor_copy(identb[:], identf[:])
                v.tensor_copy(maskb[:], maskf).then_inc(n, 1)
                v.memset(kp[KROWS:SROWS, :, :], 1.0)
                v.tensor_copy(pickb[:], pickf).then_inc(n, 1)
                dve.wait_ge(s_setup["pe"], 6)
                src = st[1][:].rearrange("p (c n) -> p c n", c=KC)
                v.tensor_reduce(r_abs[:, 0, :], src, AX.X, ALU.max, apply_absolute_value=True).then_inc(n, 1)
                dve.wait_ge(n, 4)
                v.tensor_scalar(r_abs[:, 1, :], r_abs[:, 0, :], 1e-12, 1.0 / INT8_MAX, ALU.max, ALU.mult).then_inc(n, 1)
                dve.wait_ge(n, 5)
                v.reciprocal(r_abs[:, 2, :], r_abs[:, 1, :]).then_inc(n, 1)
                dve.wait_ge(n, 6)
                for c in range(KC):
                    v.tensor_scalar(rhs_t[:, c, :], src[:, c, :], r_abs[:, 2, c:c + 1], INT8_MAX, ALU.mult, ALU.min)
                    last = v.tensor_scalar(r_diag[:, c, :], identf[:], r_abs[:, 1, c:c + 1], None, ALU.mult)
                last.then_inc(n, 1)
                dve.wait_ge(n, 7)
                v.tensor_scalar(rhs_t, rhs_t, -INT8_MAX, MAGIC, ALU.max, ALU.add).then_inc(side, 1)
                dve.wait_ge(side, 1)
                v.tensor_scalar(rq_t, rhs_t, MAGIC, None, ALU.subtract).then_inc(n, 1)
                v.tensor_copy(b_2p[:, 0, :], b_2).then_inc(side, 1)
                dve.wait_ge(side, 2)
                v.tensor_tensor(b_2r, b_2, b_2p[:, 0, :], ALU.subtract).then_inc(n, 1)
                dve.wait_ge(n, 9)
                v.tensor_copy(b_2p[:, 1, :], b_2r).then_inc(n, 1)
                dve.wait_ge(n, 10)
                v.tensor_tensor(b_2p[:, 2, :], b_2r, b_2p[:, 1, :], ALU.subtract).then_inc(n, 1)
                dve.wait_ge(s_setup["act"], 6)
                for c in range(KC):
                    for e in range(E):
                        v.tensor_scalar(w_1s[:, c, e * HID:(e + 1) * HID], w_1[:, c, e, :],
                                        lnt[:, 0, c, e:e + 1], None, ALU.mult)
                v.tensor_tensor(b_1[:], b_1[:], b_1e[:], ALU.add).then_inc(n, 1)
                dve.wait_ge(s_setup["act"], 8)
                dve.wait_ge(s_setup["pool"], 7)

            def scan(s, layer, b):
                need(dve, s_x, b, 16)
                for other in range(2):
                    need(dve, s_low[other], cut_before(0, b, other), 0)
                v.tensor_scalar(xs, xin, ALPHA, None, ALU.mult).then_inc(s_xs.sem, 1)
                need(dve, s_xs, b, 1)
                factor = decay[:].broadcast_to([128, T - 1])
                v.tensor_tensor_scan(fwd[:, 1:T], factor, xs[:, 1:T], xin[:, 0:1],
                                     ALU.mult, ALU.add).then_inc(s_scan.sem, 1)
                v.tensor_tensor_scan(bwd[:, 0:T - 1][:, ::-1], factor, xs[:, 0:T - 1][:, ::-1],
                                     xin[:, T - 1:T], ALU.mult, ALU.add).then_inc(s_scan.sem, 1)
                v.tensor_copy(fwd[:, 0:1], xin[:, 0:1])
                v.tensor_copy(bwd[:, T - 1:T], xin[:, T - 1:T]).then_inc(s_scan.sem, 1)
                need(dve, s_scan, b, 3)
                v.tensor_tensor(fwd, fwd, bwd, ALU.add).then_inc(s_ewma.sem, 1)

            def tok(s, layer, b, n):
                o = await_full(dve, s.key)
                if n == 0:
                    if b.k or b.c > 2:
                        need(dve, s_stored, b + -3, 16)
                    if b.k or b.c > 1:
                        need(dve, s_stashed[1], b + -2, 16)
                    need(dve, s_stashed[0], b, 0)
                consumed(dve, v.tensor_tensor(res[:, 2 * n:2 * n + 2, :], o[0:TB, 0, :].rearrange("p (t d) -> p t d", t=2),
                                              b_tok[:].unsqueeze(1).broadcast_to([TB, 2, D]), ALU.add), s)

            def source(n):
                return (xn if n == 2 else res), (xh if n == 2 else xn)

            def stats_(s, layer, b, n, half):
                src, _ = source(n)
                blocks = range(3 * half, 3 * half + 3)
                wrote_res = {0: ("tok", 0, 2), 1: ("wo", 0, 2), 3: ("w2", 0, NT - 1), 4: ("wo", 1, 2)}
                if half == 0 and n in wrote_res:
                    await_done(dve, wrote_res[n])
                for t in blocks:
                    if n == 2:
                        need(dve, s_norm[1], b, t + 1)
                    last = v.bn_stats(stats[:, t, :], src[:, t, :])
                if half == 0:
                    return
                last.then_inc(s_stats[n].sem, 1)
                need(dve, s_stats[n], b, 1)
                stand_apart(dve)
                for t in range(NT):
                    last = v.bn_aggr(mv[:, t, :], stats[:, t, :])
                last.then_inc(s_mv[n].sem, 1)

            def apply(s, layer, b, n, half):
                src, dst = source(n)
                need(dve, s_rstd[n], b, 1)
                for t in range(3 * half, 3 * half + 3):
                    v.tensor_scalar(dst[:, t, :], src[:, t, :], mv[:, t, 0:1], rstd[:, t:t + 1],
                                    ALU.subtract, ALU.mult).then_inc(s_norm[n].sem, 1)

            def add_to_res(s, n, per):
                o = await_full(dve, s.key)
                r = res[:, n * per:(n + 1) * per, :].rearrange("p t d -> p (t d)")
                consumed(dve, v.tensor_tensor(r, o[0:TB, 0, 0:per * D], r, ALU.add), s)

            def wo(s, layer, b, n):
                need(dve, s_fetched[layer], b, 16)
                add_to_res(s, n, 2)

            def qk(s, layer, b, w, c, half):
                o = await_full(dve, s.key)
                n = (w * KC + c) * 2 + half + 1
                need(dve, s_high[layer], b, n)
                if half == 0 and w == 1:
                    need(dve, s_low[layer], b, c + 1)
                if half == 0 and w == 0:
                    for other in range(2):
                        need(dve, s_low[other], cut_before(layer, b, other), 0)
                cols = slice(half * HALF, (half + 1) * HALF)
                consumed(dve, v.tensor_tensor(rest[:, c, cols], o[:, 0, 0:HALF], parts[:, c, 0, cols], ALU.subtract), s)
                await_done(dve, s.key)
                v.tensor_copy(parts[:, c, 1, cols], rest[:, c, cols]).then_inc(s_mid[layer].sem, 1)

            def low(s, layer, b, w, c):
                need(dve, s_mid[layer], b, (w * KC + c + 1) * 2)
                v.tensor_tensor(parts[:, c, 2, :], rest[:, c, :], parts[:, c, 1, :],
                                ALU.subtract).then_inc(s_low[layer].sem, 1)

            def max_(s, layer, b, g, u):
                i, h0, nh, k0, n = MAX_UNITS[u]
                o = await_full(dve, s.key)
                to = mx[:, g % 2, h0:h0 + nh, i] if i < SPLIT else mx2[:, h0, i - SPLIT, min(k0, 1):min(k0, 1) + 1]
                consumed(dve, v.tensor_reduce(to, o[0:TB, 0, 0:nh * n].rearrange("p (h t) -> p h t", h=nh),
                                              AX.X, ALU.max), s)
                if u == len(MAX_UNITS) - 1:
                    split_maxima(s, layer, number(layer, b), g)

            def split_maxima(s, layer, a, g):
                await_done(dve, s.key)
                v.tensor_tensor(mx[:, g % 2, :, SPLIT:NT], mx2[:, :, :, 0], mx2[:, :, :, 1], ALU.max)\
                    .then_inc(s_ms.sem, 1)
                m = mx[:, g % 2].rearrange("p h i -> p (h i)")
                need(dve, s_ms, a, g * 5 + 1)
                v.tensor_scalar(ms[:, g % 2, 0, :], m, -1.0, None, ALU.mult).then_inc(s_ms.sem, 1)
                need(dve, s_ms, a, g * 5 + 2)
                v.scalar_tensor_tensor(out=mr[:], in0=m, scalar=-1.0, in1=ms[:, g % 2, 0, :],
                                       op0=ALU.mult, op1=ALU.subtract).then_inc(s_ms.sem, 1)
                need(dve, s_ms, a, g * 5 + 3)
                v.tensor_copy(ms[:, g % 2, 1, :], mr[:]).then_inc(s_ms.sem, 1)
                need(dve, s_ms, a, g * 5 + 4)
                v.tensor_tensor(ms[:, g % 2, 2, :], mr[:], ms[:, g % 2, 1, :], ALU.subtract).then_inc(s_ms.sem, 1)

            def turn_(s, layer, b, g, half):
                o = await_full(dve, s.key)
                if g > 0:
                    await_done(dve, ("turn", layer, g - 1, half))
                ov = o[0:TB, 0, 0:384].rearrange("p (t h f) -> p t h f", t=3, h=GH)
                blocks = slice(3 * half, 3 * half + 3)
                v.reciprocal(rden[:, blocks, :], ov[:, :, :, DH]).then_inc(s_rden.sem, 1)
                need(dve, s_rden, number(layer, b), 2 * g + half + 1)
                consumed(dve, v.tensor_tensor(
                    ao[layer][:, blocks, g * 64:(g + 1) * 64].rearrange("p t (h d) -> p t h d", h=GH),
                    ov[:, :, :, 0:DH], rden[:, blocks, :].unsqueeze(3).broadcast_to([TB, 3, GH, DH]), ALU.mult), s)

            def logit(s, layer, b):
                o = await_full(dve, s.key)
                consumed(dve, v.tensor_copy(lg[:], o[0:TB, 0, 0:NT * E].rearrange("p (t e) -> p t e", t=NT)), s)

            def gate(s, layer, b):
                await_done(dve, ("logit", 0))
                v.tensor_reduce(lgm[:, 0, :], lg[:], AX.X, ALU.max).then_inc(s_gate.sem, 1)
                need(dve, s_gate, b, 1)
                v.tensor_tensor(sel[:], lg[:], lgm[:, 0, :].unsqueeze(2).broadcast_to([TB, NT, E]), ALU.is_equal)\
                    .then_inc(s_gate.sem, 1)
                need(dve, s_gate, b, 2)
                v.tensor_tensor(sel[:], sel[:], rank[:].unsqueeze(1).broadcast_to([TB, NT, E]), ALU.mult)\
                    .then_inc(s_gate.sem, 1)
                need(dve, s_gate, b, 3)
                v.tensor_reduce(lgm[:, 1, :], sel[:], AX.X, ALU.max).then_inc(s_gate.sem, 1)
                need(dve, s_gate, b, 4)
                v.tensor_tensor(sel[:], sel[:], lgm[:, 1, :].unsqueeze(2).broadcast_to([TB, NT, E]), ALU.is_equal)\
                    .then_inc(s_gate.sem, 1)
                need(dve, s_gate, b, 5)
                for r in range(3):
                    last = v.tensor_copy(mk[:, :, r * E:(r + 1) * E], sel[:])
                last.then_inc(s_mk.sem, 1)
                v.tensor_scalar(mk[:, :, 3 * E:4 * E], sel[:], -NEG, NEG, ALU.mult, ALU.add).then_inc(s_mk.sem, 1)

            def qktok(s, layer, b, t):
                o = await_full(dve, s.key)
                if t > 1:
                    need(dve, s_qr, b, t - 1)
                v.tensor_tensor(qr[:, t, :].rearrange("p (h d) -> p h d", d=DH),
                                o[0:TB, 0, :].rearrange("p (h d) -> p h d", d=DH),
                                cos_sb[:, t, :].unsqueeze(1).broadcast_to([TB, 2 * H, DH]), ALU.mult)
                pairs = "p (h f two) -> p h f two"
                consumed(dve, v.tensor_tensor(
                    rot[:, t % 2, :].rearrange(pairs, f=DH // 2, two=2),
                    o[0:TB, 0, :].rearrange(pairs, f=DH // 2, two=2)[:, :, :, ::-1],
                    sin_sb[:, t, :].rearrange("p (f two) -> p f two", two=2).unsqueeze(1)
                    .broadcast_to([TB, 2 * H, DH // 2, 2]), ALU.mult), s)
                await_done(dve, s.key)
                v.tensor_tensor(qr[:, t, :], qr[:, t, :], rot[:, t % 2, :], ALU.add).then_inc(s_qr.sem, 1)

            def quant(s, layer, b, n):
                (quant_scale, quant_product, quant_round)[n](b)

            def quant_scale(b):
                need(dve, s_norm[4], b, NT)
                v.tensor_reduce(am[:, 0, :], xn[:], AX.X, ALU.max, apply_absolute_value=True).then_inc(s_amax.sem, 1)
                need(dve, s_amax, b, 1)
                v.tensor_scalar(am[:, 1, :], am[:, 0, :], 1e-12, 1.0 / INT8_MAX, ALU.max, ALU.mult).then_inc(s_amax.sem, 1)
                need(dve, s_amax, b, 2)
                v.reciprocal(am[:, 2, :], am[:, 1, :]).then_inc(s_amax.sem, 1)

            def quant_product(b):
                need(dve, s_amax, b, 3)
                for t in range(NT):
                    v.tensor_scalar(xh[:, t, :], xn[:, t, :], am[:, 2, t:t + 1], INT8_MAX, ALU.mult, ALU.min)\
                        .then_inc(s_quant.sem, 1)

            def quant_round(b):
                need(dve, s_quant, b, NT)
                v.tensor_scalar(xh[:], xh[:], -INT8_MAX, MAGIC, ALU.max, ALU.add).then_inc(s_quant.sem, 1)
                need(dve, s_quant, b, NT + 1)
                v.tensor_scalar(qb, xh[:], MAGIC, None, ALU.subtract).then_inc(s_quant.sem, 1)

            def ffn(s, layer, b, n):
                o = await_full(dve, s.key)
                for j in range(2):
                    t = n * 2 + j
                    last = v.scalar_tensor_tensor(out=xh[:, t, :], in0=o[0:TB, 0, j * D:(j + 1) * D],
                                                  scalar=am[:, 1, t:t + 1], in1=r_scale[:],
                                                  op0=ALU.mult, op1=ALU.mult)
                consumed(dve, last, s)

            def store(s, layer, b):
                await_done(dve, *[("ffn", 1, n) for n in range(3)])
                v.tensor_tensor(res[:], res[:], xh[:], ALU.add).then_inc(s_out.sem, 1)

            dve.wait_ge(s_setup["pool"], 1)
            walk(dve, {"setup": setup, "scan": scan, "tok": tok, "stats": stats_, "apply": apply, "wo": wo,
                       "w2": lambda s, layer, b, t: add_to_res(s, t, 1), "qk": qk, "low": low, "max": max_, "turn": turn_,
                       "logit": logit, "gate": gate, "qktok": qktok, "quant": quant, "ffn": ffn, "store": store})


_IN = ['x', 'L0_tok_W', 'L0_tok_b', 'L0_attn_Wqvk', 'L0_attn_Wo', 'L0_ffn_Wg', 'L0_ffn_ln_scale', 'L0_ffn_ln_bias',
       'L0_ffn_W1', 'L0_ffn_b1', 'L0_ffn_W2', 'L0_ffn_b2', 'L1_attn_Wqkv', 'L1_attn_Wo', 'L1_ffn_rhs']


def _tables():
    pos = np.arange(T, dtype=np.float32)
    freqs = np.exp(np.float32(-np.log(10000.0)) * np.arange(0, DH, 2, dtype=np.float32) / np.float32(DH))
    angles = np.repeat(pos[:, None] * freqs.astype(np.float32)[None, :], 2, axis=-1)
    sign = np.tile(np.array([-1.0, 1.0], np.float32), DH // 2)
    causal = np.where(np.arange(TB)[None, :] > np.arange(TB)[:, None], np.float32(NEG), np.float32(0.0))
    pick = np.zeros((32, 4, 128), np.float32)
    for e in range(E):
        pick[3 * E + e, e // 2, e % 2 * HID:(e % 2 + 1) * HID] = 1.0
    return {
        "ident": np.eye(128, dtype=np.float32), "causal": causal.astype(np.float32),
        "cosines": np.cos(angles).astype(np.float32), "sines": (np.sin(angles) * sign).astype(np.float32),
        "pick": pick,
    }


def kernel(**inputs):
    import concourse.bacc as _bacc
    from concourse.bass_utils import run_bass_kernel_spmd as _run

    nc = _bacc.Bacc("TRN2", target_bir_lowering=False, num_devices=1)
    arrays = {f"in_{n}": np.ascontiguousarray(inputs[n]) for n in _IN}
    arrays |= {f"table_{n}": a for n, a in _tables().items()}
    args = [nc.dram_tensor(n, a.shape, mybir.dt.from_np(a.dtype), kind="ExternalInput").ap() for n, a in arrays.items()]
    out = nc.dram_tensor("out", (B, T, D), F32, kind="ExternalOutput").ap()
    tower(nc, *args, out)
    r = _run(nc, [arrays], core_ids=[0])
    return r.results[0]["out"]
```
